# Optimizing a Trainium2 kernel written in Bass

```python
import numpy as np
import jax
import jax.numpy as jnp

def _softmax(x, axis=-1):
    return jax.nn.softmax(x, axis=axis)

def _gelu(x):
    return jax.nn.gelu(x, approximate=True)

def _silu(x):
    return jax.nn.silu(x)

def _sigmoid(x):
    return jax.nn.sigmoid(x)

def _layernorm(x, axis=-1, eps=1e-05):
    m = jnp.mean(x, axis=axis, keepdims=True)
    v = jnp.var(x, axis=axis, keepdims=True)
    return (x - m) / jnp.sqrt(v + eps)

def _scatter_add(tgt, idx, src, axis=0):
    return tgt.at[idx].add(src)

def _segment_sum(src, seg, n):
    return jax.ops.segment_sum(src, seg, n)
kernel_name = 'mk_dlrm_tower_d1_rec_r8_656ded'

def setup_inputs(seed: int=0):
    np.random.seed(seed)
    _w = jnp.asarray

    def _rec_inputs():
        import jax
        import jax.numpy as jnp
        _tk = jax.random.key(seed)
        dense_ctx = jax.random.normal(jax.random.fold_in(_tk, 190), (512, 16), jnp.float32)
        ids = jnp.stack([jax.random.randint(jax.random.fold_in(_tk, 200 + f), (512,), 0, v, jnp.int32) for f, v in enumerate([1250, 125000, 12500, 125000, 1000, 125000, 1000, 12500, 12500, 1250, 1000, 1000, 1250, 1250, 125000, 1000, 125000, 1000, 125000, 1250, 125000, 12500, 1000, 1250, 12500, 12500])], axis=1)
        tbl_0 = 0.05 * jax.random.normal(jax.random.fold_in(_tk, 500 + 0), (1250, 32), jnp.float32)
        tbl_1 = 0.05 * jax.random.normal(jax.random.fold_in(_tk, 500 + 1), (125000, 32), jnp.float32)
        tbl_2 = 0.05 * jax.random.normal(jax.random.fold_in(_tk, 500 + 2), (12500, 32), jnp.float32)
        tbl_3 = 0.05 * jax.random.normal(jax.random.fold_in(_tk, 500 + 3), (125000, 32), jnp.float32)
        tbl_4 = 0.05 * jax.random.normal(jax.random.fold_in(_tk, 500 + 4), (1000, 32), jnp.float32)
        tbl_5 = 0.05 * jax.random.normal(jax.random.fold_in(_tk, 500 + 5), (125000, 32), jnp.float32)
        tbl_6 = 0.05 * jax.random.normal(jax.random.fold_in(_tk, 500 + 6), (1000, 32), jnp.float32)
        tbl_7 = 0.05 * jax.random.normal(jax.random.fold_in(_tk, 500 + 7), (12500, 32), jnp.float32)
        tbl_8 = 0.05 * jax.random.normal(jax.random.fold_in(_tk, 500 + 8), (12500, 32), jnp.float32)
        tbl_9 = 0.05 * jax.random.normal(jax.random.fold_in(_tk, 500 + 9), (1250, 32), jnp.float32)
        tbl_10 = 0.05 * jax.random.normal(jax.random.fold_in(_tk, 500 + 10), (1000, 32), jnp.float32)
        tbl_11 = 0.05 * jax.random.normal(jax.random.fold_in(_tk, 500 + 11), (1000, 32), jnp.float32)
        tbl_12 = 0.05 * jax.random.normal(jax.random.fold_in(_tk, 500 + 12), (1250, 32), jnp.float32)
        tbl_13 = 0.05 * jax.random.normal(jax.random.fold_in(_tk, 500 + 13), (1250, 32), jnp.float32)
        tbl_14 = 0.05 * jax.random.normal(jax.random.fold_in(_tk, 500 + 14), (125000, 32), jnp.float32)
        tbl_15 = 0.05 * jax.random.normal(jax.random.fold_in(_tk, 500 + 15), (1000, 32), jnp.float32)
        tbl_16 = 0.05 * jax.random.normal(jax.random.fold_in(_tk, 500 + 16), (125000, 32), jnp.float32)
        tbl_17 = 0.05 * jax.random.normal(jax.random.fold_in(_tk, 500 + 17), (1000, 32), jnp.float32)
        tbl_18 = 0.05 * jax.random.normal(jax.random.fold_in(_tk, 500 + 18), (125000, 32), jnp.float32)
        tbl_19 = 0.05 * jax.random.normal(jax.random.fold_in(_tk, 500 + 19), (1250, 32), jnp.float32)
        tbl_20 = 0.05 * jax.random.normal(jax.random.fold_in(_tk, 500 + 20), (125000, 32), jnp.float32)
        tbl_21 = 0.05 * jax.random.normal(jax.random.fold_in(_tk, 500 + 21), (12500, 32), jnp.float32)
        tbl_22 = 0.05 * jax.random.normal(jax.random.fold_in(_tk, 500 + 22), (1000, 32), jnp.float32)
        tbl_23 = 0.05 * jax.random.normal(jax.random.fold_in(_tk, 500 + 23), (1250, 32), jnp.float32)
        tbl_24 = 0.05 * jax.random.normal(jax.random.fold_in(_tk, 500 + 24), (12500, 32), jnp.float32)
        tbl_25 = 0.05 * jax.random.normal(jax.random.fold_in(_tk, 500 + 25), (12500, 32), jnp.float32)
        _rk = jax.random.fold_in(_tk, 7)
        W_top1 = 0.0606339 * jax.random.normal(jax.random.fold_in(_tk, 801), (272, 512), jnp.float32)
        W_top2 = 0.0441942 * jax.random.normal(jax.random.fold_in(_tk, 802), (512, 256), jnp.float32)
        W_top3 = 0.0625 * jax.random.normal(jax.random.fold_in(_tk, 803), (256, 1), jnp.float32)
        b_top1 = jnp.zeros((512,), jnp.float32)
        b_top2 = jnp.zeros((256,), jnp.float32)
        return (dense_ctx, ids, tbl_0, tbl_1, tbl_2, tbl_3, tbl_4, tbl_5, tbl_6, tbl_7, tbl_8, tbl_9, tbl_10, tbl_11, tbl_12, tbl_13, tbl_14, tbl_15, tbl_16, tbl_17, tbl_18, tbl_19, tbl_20, tbl_21, tbl_22, tbl_23, tbl_24, tbl_25, W_top1, b_top1, W_top2, b_top2, W_top3)
    dense_ctx, ids, tbl_0, tbl_1, tbl_2, tbl_3, tbl_4, tbl_5, tbl_6, tbl_7, tbl_8, tbl_9, tbl_10, tbl_11, tbl_12, tbl_13, tbl_14, tbl_15, tbl_16, tbl_17, tbl_18, tbl_19, tbl_20, tbl_21, tbl_22, tbl_23, tbl_24, tbl_25, W_top1, b_top1, W_top2, b_top2, W_top3 = _rec_inputs()

    def _L0_rec_setup():
        import jax, jax.numpy as jnp
        import numpy as np
        M_FIELDS = 26
        H1 = 128
        H2 = 128
        BATCH = 256
        EMB_K = 32

        def _cin_layer(x_prev, x0, W, b):
            return jnp.einsum('bik,bjk,hij->bhk', x_prev, x0, W) + b[None, :, None]
        key = jax.random.key(seed)
        k0, k1, k2, k3, k4 = jax.random.split(key, 5)
        inputs = jax.random.normal(k0, (BATCH, M_FIELDS, EMB_K), dtype=jnp.float32)
        W1 = jax.random.normal(k1, (H1, M_FIELDS, M_FIELDS), dtype=jnp.float32) * 0.05
        b1 = jax.random.normal(k2, (H1,), dtype=jnp.float32) * 0.05
        W2 = jax.random.normal(k3, (H2, H1, M_FIELDS), dtype=jnp.float32) * 0.05
        b2 = jax.random.normal(k4, (H2,), dtype=jnp.float32) * 0.05
        return {'inputs': inputs, 'W1': W1, 'b1': b1, 'W2': W2, 'b2': b2}
    _L0_rec_all = _L0_rec_setup()
    _L0_rec_in = {k: v for k, v in _L0_rec_all.items() if k in ('W1', 'b1', 'W2', 'b2')}
    del _L0_rec_all
    return {'dense_ctx': dense_ctx, 'ids': ids, 'tbl_0': tbl_0, 'tbl_1': tbl_1, 'tbl_2': tbl_2, 'tbl_3': tbl_3, 'tbl_4': tbl_4, 'tbl_5': tbl_5, 'tbl_6': tbl_6, 'tbl_7': tbl_7, 'tbl_8': tbl_8, 'tbl_9': tbl_9, 'tbl_10': tbl_10, 'tbl_11': tbl_11, 'tbl_12': tbl_12, 'tbl_13': tbl_13, 'tbl_14': tbl_14, 'tbl_15': tbl_15, 'tbl_16': tbl_16, 'tbl_17': tbl_17, 'tbl_18': tbl_18, 'tbl_19': tbl_19, 'tbl_20': tbl_20, 'tbl_21': tbl_21, 'tbl_22': tbl_22, 'tbl_23': tbl_23, 'tbl_24': tbl_24, 'tbl_25': tbl_25, 'W_top1': W_top1, 'b_top1': b_top1, 'W_top2': W_top2, 'b_top2': b_top2, 'W_top3': W_top3, 'L0_rec_W1': _L0_rec_in['W1'], 'L0_rec_b1': _L0_rec_in['b1'], 'L0_rec_W2': _L0_rec_in['W2'], 'L0_rec_b2': _L0_rec_in['b2']}

def reference(dense_ctx, ids, tbl_0, tbl_1, tbl_2, tbl_3, tbl_4, tbl_5, tbl_6, tbl_7, tbl_8, tbl_9, tbl_10, tbl_11, tbl_12, tbl_13, tbl_14, tbl_15, tbl_16, tbl_17, tbl_18, tbl_19, tbl_20, tbl_21, tbl_22, tbl_23, tbl_24, tbl_25, W_top1, b_top1, W_top2, b_top2, W_top3, L0_rec_W1, L0_rec_b1, L0_rec_W2, L0_rec_b2):
    import jax
    import jax.numpy as jnp

    def _L0_rec_ref(inputs, W1, b1, W2, b2):
        import jax, jax.numpy as jnp
        import numpy as np
        M_FIELDS = 26
        H1 = 128
        H2 = 128
        BATCH = 256
        EMB_K = 32

        def _cin_layer(x_prev, x0, W, b):
            return jnp.einsum('bik,bjk,hij->bhk', x_prev, x0, W) + b[None, :, None]
        x1 = _cin_layer(inputs, inputs, W1, b1)
        x2 = _cin_layer(x1, inputs, W2, b2)
        res = jnp.concatenate([x1, x2], axis=1)
        return jnp.sum(res, axis=-1)
    e = jnp.stack([tbl_0[ids[:, 0]], tbl_1[ids[:, 1]], tbl_2[ids[:, 2]], tbl_3[ids[:, 3]], tbl_4[ids[:, 4]], tbl_5[ids[:, 5]], tbl_6[ids[:, 6]], tbl_7[ids[:, 7]], tbl_8[ids[:, 8]], tbl_9[ids[:, 9]], tbl_10[ids[:, 10]], tbl_11[ids[:, 11]], tbl_12[ids[:, 12]], tbl_13[ids[:, 13]], tbl_14[ids[:, 14]], tbl_15[ids[:, 15]], tbl_16[ids[:, 16]], tbl_17[ids[:, 17]], tbl_18[ids[:, 18]], tbl_19[ids[:, 19]], tbl_20[ids[:, 20]], tbl_21[ids[:, 21]], tbl_22[ids[:, 22]], tbl_23[ids[:, 23]], tbl_24[ids[:, 24]], tbl_25[ids[:, 25]]], axis=1)
    z = _L0_rec_ref(e, L0_rec_W1, L0_rec_b1, L0_rec_W2, L0_rec_b2)
    z = z.reshape(z.shape[0], -1)
    h = jnp.concatenate([z, dense_ctx], axis=1)
    h = jnp.maximum(h @ W_top1 + b_top1, 0.0)
    h = jnp.maximum(h @ W_top2 + b_top2, 0.0)
    y = h @ W_top3
    return y

_drawn_inputs = setup_inputs


def setup_inputs(seed=0):
    import zlib

    import numpy as np

    out = dict(_drawn_inputs(seed))
    spreads = {'b_top1': (0.0, 0.8), 'b_top2': (0.0, 0.8)}
    factors = {'tbl_0': 8.0,
     'tbl_1': 8.0,
     'tbl_2': 8.0,
     'tbl_3': 8.0,
     'tbl_4': 8.0,
     'tbl_5': 8.0,
     'tbl_6': 8.0,
     'tbl_7': 8.0,
     'tbl_8': 8.0,
     'tbl_9': 8.0,
     'tbl_10': 8.0,
     'tbl_11': 8.0,
     'tbl_12': 8.0,
     'tbl_13': 8.0,
     'tbl_14': 8.0,
     'tbl_15': 8.0,
     'tbl_16': 8.0,
     'tbl_17': 8.0,
     'tbl_18': 8.0,
     'tbl_19': 8.0,
     'tbl_20': 8.0,
     'tbl_21': 7.699,
     'tbl_22': 8.0,
     'tbl_23': 8.0,
     'tbl_24': 8.0,
     'tbl_25': 8.0,
     'L0_rec_W1': 7.937,
     'L0_rec_W2': 4.169,
     'dense_ctx': 5.189}
    for name, (base, spread) in spreads.items():
        noise = np.random.default_rng([zlib.crc32(name.encode()), seed]).standard_normal(out[name].shape)
        drawn = base * np.exp(spread * noise) if base else spread * noise
        out[name] = jnp.asarray(drawn.astype(out[name].dtype))
    for name, factor in factors.items():
        out[name] = (out[name] * factor).astype(out[name].dtype)
    return out
```

```python
import concourse.bass as bass
from concourse import mybir
from contextlib import ExitStack

BATCH = 512
FIELDS = 26
EMB = 32
H = 128
DENSE = 16
TOP1, TOP2 = 512, 256

P = 128
TILES = BATCH // P
GROUPS = P // EMB
SLOTS = P // GROUPS
COLS = FIELDS + 1
BD_W = GROUPS * COLS
PER_BANK = 4
BANKS = 4
RUNS = SLOTS // PER_BANK

PAIR_J = [range(0, 15), range(15, 21), range(21, 26)]
PAIR_TILES = len(PAIR_J)
FIRST = [sum(j + 1 for j in range(js[0])) for js in PAIR_J]
COUNT = [sum(j + 1 for j in js) for js in PAIR_J]
ROWS = [COUNT[0] + 1, COUNT[1], COUNT[2]]
ONE_ROW = COUNT[0]
START = [0, ROWS[0], ROWS[0] + ROWS[1]]
ALL_ROWS = sum(ROWS)

L_CHUNK = 4
L_CHUNKS = -(-FIELDS // L_CHUNK)

BT1_AT = 0
BT2_AT = BT1_AT + TOP1 // P
WT3_AT = BT2_AT + TOP2 // P
B1_AT = WT3_AT + TOP2 // P
B2_AT = B1_AT + 1
VECS = B2_AT + 1


def row_of(t, j):
    return START[t] + j * (j + 1) // 2 - FIRST[t]


def build(nc, ids, tables, dense, w1, b1, w2, b2, wt1, bt1, wt2, bt2, wt3, out):
    fp32, int32 = mybir.dt.float32, mybir.dt.int32
    ALU = mybir.AluOpType
    ACT = mybir.ActivationFunctionType

    ctx = ExitStack()
    with ctx:
        def sb(name, shape, dt=fp32):
            return ctx.enter_context(nc.sbuf_tensor(name, shape, dt))

        def sem(name):
            return ctx.enter_context(nc.semaphore(name))

        idx = sb("idx", [P, TILES * FIELDS], int32)
        w1_sb = sb("w1_sb", [H, FIELDS, FIELDS])
        w2_sb = sb("w2_sb", [H, H, FIELDS])
        vec_sb = sb("vec_sb", [VECS, P])
        dense_sb = sb("dense_sb", [P, TILES, DENSE])
        wt1_sb = sb("wt1_sb", [H, 2, TOP1])
        wt1d_sb = sb("wt1d_sb", [DENSE, TOP1])
        wt2_sb = sb("wt2_sb", [P, TOP1 // P, TOP2])

        ident = sb("ident", [P, P])
        w1s = sb("w1s", [H, ALL_ROWS])
        w1p = sb("w1p", [P, PAIR_TILES, H])
        w2t = sb("w2t", [H, FIELDS, H])
        fold = sb("fold", [P, PAIR_TILES, FIELDS, H])
        b2x = sb("b2x", [H, 1])
        dense_t = sb("dense_t", [DENSE, BATCH])
        vec_t = sb("vec_t", [P, VECS])
        bt1_sb, bt2_sb = vec_t[:, BT1_AT:BT2_AT], vec_t[:, BT2_AT:WT3_AT]
        wt3_sb, b1_sb, b2_sb = vec_t[:, WT3_AT:B1_AT], vec_t[:, B1_AT:B2_AT], vec_t[:, B2_AT:VECS]

        emb = sb("emb", [P, 2, FIELDS * EMB])
        emb_t = sb("emb_t", [P, FIELDS, SLOTS])
        pairs = sb("pairs", [P, ALL_ROWS, SLOTS])
        diag = sb("diag", [P, SLOTS, GROUPS, COLS])
        triples = sb("triples", [P, PAIR_TILES, COLS, P])
        z_sb = sb("z_sb", [H, 2, P])
        h1_sb = sb("h1_sb", [P, TOP1 // P, P])
        h2_sb = sb("h2_sb", [P, TOP2 // P, P])
        y_sb = sb("y_sb", [1, BATCH])

        tri_ps = ctx.enter_context(nc.psum_tensor("tri_ps", [P, BANKS, 512], fp32))
        z_ps = ctx.enter_context(nc.psum_tensor("z_ps", [P, 512], fp32))
        h1_ps = ctx.enter_context(nc.psum_tensor("h1_ps", [P, 512], fp32))
        h2_ps = ctx.enter_context(nc.psum_tensor("h2_ps", [P, 512], fp32))
        y_ps = ctx.enter_context(nc.psum_tensor("y_ps", [P, 512], fp32))

        ids_in = sem("ids_in")
        w1_in = sem("w1_in")
        w2_in = sem("w2_in")
        top_in = sem("top_in")
        dense_in = sem("dense_in")
        vecs_in = sem("vecs_in")
        emb_in = [sem(f"emb_in{f}") for f in range(FIELDS)]
        ident_made = sem("ident_made")
        cleared = sem("cleared")
        halved = sem("halved")
        w1s_made = sem("w1s_made")
        b1_put = sem("b1_put")
        trans_ps = sem("trans_ps")
        trans_used = sem("trans_used")
        fold_ps = sem("fold_ps")
        fold_used = sem("fold_used")
        emb_ready = sem("emb_ready")
        diag_ready = sem("diag_ready")
        pairs_ready = sem("pairs_ready")
        tri_ready = sem("tri_ready")
        tri_used = sem("tri_used")
        z_ready, z_used = sem("z_ready"), sem("z_used")
        h1_ready, h1_used = sem("h1_ready"), sem("h1_used")
        h2_ready, h2_used = sem("h2_ready"), sem("h2_used")
        y_ready, y_used = sem("y_ready"), sem("y_used")
        y_out = sem("y_out")

        TRANS = L_CHUNKS + 2
        VECS_AT = 3 * P
        FOLDS = PAIR_TILES * L_CHUNKS

        block = ctx.enter_context(nc.Block())

        @block.sync
        def _(sp):
            sp.dma_start(idx[:].rearrange("p (t f) -> p t f", f=FIELDS),
                         ids.rearrange("(t p) f -> p t f", p=P)).then_inc(ids_in, 16)
            sp.dma_start(w2_sb[:], w2).then_inc(w2_in, 16)
            sp.dma_start(wt2_sb[:], wt2.rearrange("(c p) n -> p c n", p=P)).then_inc(top_in, 16)
            sp.dma_start(wt1_sb[:], wt1[0:2 * H, :].rearrange("(c p) n -> p c n", p=H)).then_inc(top_in, 16)
            sp.dma_start(wt1d_sb[:], wt1[2 * H:2 * H + DENSE, :]).then_inc(top_in, 16)
            sp.wait_ge(y_used, TILES)
            sp.dma_start(out.rearrange("b x -> x b"), y_sb[:]).then_inc(y_out, 16)
            sp.wait_ge(y_out, 16)

        @block.gpsimd
        def _(pool):
            nc.gpsimd.memset(ident[:], 0.0).then_inc(ident_made, 1)
            pool.wait_ge(ident_made, 1)
            nc.gpsimd.affine_select(out=ident[:], in_=ident[:], compare_op=ALU.not_equal, fill=1.0, base=0,
                                    pattern=[[-1, P]], channel_multiplier=1).then_inc(ident_made, 1)
            pool.wait_ge(ids_in, 16)
            for t in range(TILES):
                if t >= 2:
                    pool.wait_ge(emb_ready, t - 1)
                for f in range(FIELDS):
                    if t:
                        pool.wait_ge(emb_in[f], 16 * t)
                    col = f * EMB
                    i = t * FIELDS + f
                    nc.gpsimd.indirect_dma_start(
                        out=emb[:, t % 2, col:col + EMB], out_offset=None, in_=tables[f],
                        in_offset=bass.IndirectOffsetOnAxis(ap=idx[:, i:i + 1], axis=0)).then_inc(emb_in[f], 16)

        @block.vector
        def _(dve):
            nc.vector.memset(diag[:], 0.0).then_inc(cleared, 1)
            nc.vector.memset(pairs[:, ONE_ROW, :], 1.0).then_inc(pairs_ready, 1)
            dve.wait_ge(cleared, 1)
            for g in range(GROUPS):
                last = nc.vector.memset(diag[EMB * g:EMB * (g + 1), :, g, FIELDS:COLS], 1.0)

            last.then_inc(diag_ready, 1)

            dve.wait_ge(w1_in, 16)
            d = w1_sb[:].rearrange("h i j -> h (i j)")[:, 0:FIELDS * FIELDS:FIELDS + 1]
            nc.vector.tensor_scalar(d, d, 0.5, None, ALU.mult).then_inc(halved, 1)
            dve.wait_ge(halved, 1)
            for t, js in enumerate(PAIR_J):
                for j in js:
                    at = row_of(t, j)
                    last = nc.vector.tensor_tensor(w1s[:, at:at + j + 1], w1_sb[:, 0:j + 1, j],
                                                   w1_sb[:, j, 0:j + 1], ALU.add)
            last.then_inc(w1s_made, 1)

            def multiply_tile(n, half):
                for f in range(FIELDS):
                    dve.wait_ge(emb_in[f], n * 16 + 16)
                dve.wait_ge(pairs_ready, n * PAIR_TILES + 1)
                dve.wait_ge(diag_ready, n + 1)
                nc.vector.transpose(emb_t[:].rearrange("p f s -> p (f s)"),
                                    emb[:, half, :]).then_inc(emb_ready, 1)
                dve.wait_ge(emb_ready, n + 1)
                for t, js in enumerate(PAIR_J):
                    dve.wait_ge(tri_ready, n * (RUNS * PAIR_TILES) + RUNS * (t + 1))
                    for j in js:
                        at = row_of(t, j)
                        last = nc.vector.tensor_tensor(
                            pairs[:, at:at + j + 1, :], emb_t[:, 0:j + 1, :],
                            emb_t[:, j:j + 1, :].broadcast_to([P, j + 1, SLOTS]), ALU.mult)
                    last.then_inc(pairs_ready, 1)
                    if t == 0:
                        dve.wait_ge(tri_ready, n * (RUNS * PAIR_TILES) + RUNS * PAIR_TILES)
                        for g in range(GROUPS):
                            rows = slice(EMB * g, EMB * (g + 1))
                            last = nc.vector.tensor_copy(diag[rows, :, g, 0:FIELDS],
                                                         emb_t[rows, :, :].rearrange("p f s -> p s f"))
                        last.then_inc(diag_ready, 1)

            with dve.Fori(0, TILES // 2) as pair:
                for half in range(2):
                    multiply_tile(pair * 2 + half, half)

        @block.tensor
        def _(pe):
            def transposed(c, parts):
                if c >= BANKS:
                    pe.wait_ge(trans_used, c - BANKS + 1)
                for o, src in parts:
                    rows, cols = src.shape[1], src.shape[0]
                    last = nc.tensor.transpose(tri_ps[0:rows, c % BANKS, o:o + cols], src, ident[0:cols, 0:cols])
                last.then_inc(trans_ps, 1)

            pe.wait_ge(ident_made, 2)
            pe.wait_ge(w2_in, 16)
            for c in range(L_CHUNKS):
                ls = range(c * L_CHUNK, min(FIELDS, (c + 1) * L_CHUNK))
                parts = [((l - ls[0]) * H, w2_sb[:, :, l]) for l in ls]
                if c == L_CHUNKS - 1:
                    pe.wait_ge(vecs_in, 80)
                    parts.append((VECS_AT, vec_sb[:]))
                transposed(c, parts)
            pe.wait_ge(dense_in, 16)
            transposed(L_CHUNKS, [(t * P, dense_sb[:, t, :]) for t in range(TILES)])
            pe.wait_ge(w1s_made, 1)
            pe.wait_ge(b1_put, 3)
            transposed(L_CHUNKS + 1, [(t * H, w1s[:, START[t]:START[t] + ROWS[t]]) for t in range(PAIR_TILES)])

            for c in range(FOLDS):
                t, lc = c // L_CHUNKS, c % L_CHUNKS
                ls = slice(lc * L_CHUNK, min(FIELDS, (lc + 1) * L_CHUNK))
                pe.wait_ge(trans_used, min(TRANS, TRANS + c - BANKS + 1) if c < BANKS else TRANS)
                if c >= BANKS:
                    pe.wait_ge(fold_used, c - BANKS + 1)
                bank = (TRANS + c) % BANKS
                n_cols = (ls.stop - ls.start) * H
                nc.tensor.matmul(tri_ps[0:ROWS[t], bank, 0:n_cols], w1s[:, START[t]:START[t] + ROWS[t]],
                                 w2t[:, ls, :], start=True, stop=True).then_inc(fold_ps, 1)
            pe.wait_ge(fold_used, FOLDS)
            pe.wait_ge(top_in, 48)

            pe.sem_inc(tri_ready, RUNS * PAIR_TILES)


            with pe.Fori(0, TILES) as n:
                for t in range(PAIR_TILES):
                    pe.wait_ge(pairs_ready, n * PAIR_TILES + (t + 2))
                    if t == 0:
                        pe.wait_ge(diag_ready, n + 2)
                    for r in range(RUNS):
                        run = t * RUNS + r
                        pe.wait_ge(tri_used, n * (RUNS * PAIR_TILES) + run + 1)
                        for q in range(PER_BANK):
                            s = r * PER_BANK + q
                            last = nc.tensor.matmul(
                                tri_ps[0:ROWS[t], run % BANKS, q * BD_W:(q + 1) * BD_W],
                                pairs[:, START[t]:START[t] + ROWS[t], s],
                                diag[:, s, :, :].rearrange("p g l -> p (g l)"), start=True, stop=True)
                        last.then_inc(tri_ready, 1)

                for t in range(PAIR_TILES):
                    pe.wait_ge(tri_used, n * (RUNS * PAIR_TILES) + BANKS + RUNS * (t + 1))
                    for l in range(FIELDS):
                        nc.tensor.matmul(z_ps[:, P:2 * P], fold[0:ROWS[t], t, l, :], triples[0:ROWS[t], t, l, :],
                                         start=(t == 0 and l == 0), stop=(t == PAIR_TILES - 1 and l == FIELDS - 1))
                for t in range(PAIR_TILES):
                    last = nc.tensor.matmul(z_ps[:, 0:P], w1p[0:ROWS[t], t, :], triples[0:ROWS[t], t, FIELDS, :],
                                            start=(t == 0), stop=(t == PAIR_TILES - 1))
                last.then_inc(z_ready, 1)

                pe.wait_ge(z_used, n + 1)
                for m in range(TOP1 // P):
                    cols = slice(m * P, (m + 1) * P)
                    nc.tensor.matmul(h1_ps[:, cols], wt1d_sb[:, cols], dense_t[:, bass.ds(n * P, P)],
                                     start=True, stop=False)
                    for c in range(2):
                        last = nc.tensor.matmul(h1_ps[:, cols], wt1_sb[:, c, cols], z_sb[:, c, :],
                                                start=False, stop=(c == 1))
                last.then_inc(h1_ready, 1)
                pe.wait_ge(h1_used, n + 1)
                for m in range(TOP2 // P):
                    cols = slice(m * P, (m + 1) * P)
                    for c in range(TOP1 // P):
                        last = nc.tensor.matmul(h2_ps[:, cols], wt2_sb[:, c, cols], h1_sb[:, c, :],
                                                start=(c == 0), stop=(c == TOP1 // P - 1))
                last.then_inc(h2_ready, 1)
                pe.wait_ge(h2_used, n + 1)
                for c in range(TOP2 // P):
                    last = nc.tensor.matmul(y_ps[0:1, 0:P], wt3_sb[:, c:c + 1], h2_sb[:, c, :],
                                            start=(c == 0), stop=(c == TOP2 // P - 1))
                last.then_inc(y_ready, 1)

        @block.scalar
        def _(act):
            act.dma_start(w1_sb[:], w1).then_inc(w1_in, 16)
            for at, v in ((BT1_AT, bt1), (BT2_AT, bt2), (WT3_AT, wt3.rearrange("n o -> (n o)")), (B1_AT, b1), (B2_AT, b2)):
                rows = v.shape[0] // P
                act.dma_start(vec_sb[at:at + rows, :], v.rearrange("(c p) -> c p", p=P)).then_inc(vecs_in, 16)
            act.dma_start(dense_sb[:], dense.rearrange("(t p) d -> p t d", p=P)).then_inc(dense_in, 16)

            for c in range(L_CHUNKS):
                ls = slice(c * L_CHUNK, min(FIELDS, (c + 1) * L_CHUNK))
                act.wait_ge(trans_ps, c + 1)
                if c == L_CHUNKS - 1:
                    vecs = tri_ps[:, c % BANKS, VECS_AT:VECS_AT + VECS]
                    nc.scalar.copy(vec_t[:], vecs).then_inc(b1_put, 1)
                    nc.scalar.copy(w1s[:, ONE_ROW:ONE_ROW + 1], vecs[:, B1_AT:B2_AT]).then_inc(b1_put, 1)
                    nc.scalar.mul(b2x[:], vecs[:, B2_AT:VECS], float(EMB)).then_inc(b1_put, 1)
                nc.scalar.copy(w2t[:, ls, :].rearrange("p l h -> p (l h)"),
                               tri_ps[:, c % BANKS, 0:(ls.stop - ls.start) * H]).then_inc(trans_used, 1)
            c = L_CHUNKS
            act.wait_ge(trans_ps, c + 1)
            nc.scalar.copy(dense_t[:], tri_ps[0:DENSE, c % BANKS, 0:BATCH]).then_inc(trans_used, 1)
            c = L_CHUNKS + 1
            act.wait_ge(trans_ps, c + 1)
            for t in range(PAIR_TILES):
                last = nc.scalar.copy(w1p[0:ROWS[t], t, :], tri_ps[0:ROWS[t], c % BANKS, t * H:(t + 1) * H])
            last.then_inc(trans_used, 1)

            for c in range(FOLDS):
                t, lc = c // L_CHUNKS, c % L_CHUNKS
                ls = slice(lc * L_CHUNK, min(FIELDS, (lc + 1) * L_CHUNK))
                act.wait_ge(fold_ps, c + 1)
                nc.scalar.copy(fold[0:ROWS[t], t, ls, :].rearrange("p l h -> p (l h)"),
                               tri_ps[0:ROWS[t], (TRANS + c) % BANKS,
                                      0:(ls.stop - ls.start) * H]).then_inc(fold_used, 1)
            act.wait_ge(fold_used, FOLDS)
            act.wait_ge(b1_put, 3)
            act.sem_inc(tri_used, BANKS)

            with act.Fori(0, TILES) as n:
                for t in range(PAIR_TILES):
                    for r in range(RUNS):
                        run = t * RUNS + r
                        act.wait_ge(tri_ready, n * (RUNS * PAIR_TILES) + RUNS * PAIR_TILES + run + 1)
                        dst = triples[0:ROWS[t], t, :, :].rearrange("p l (g s) -> p s g l", g=GROUPS)
                        nc.scalar.copy(dst[:, r * PER_BANK:(r + 1) * PER_BANK, :, :],
                                       tri_ps[0:ROWS[t], run % BANKS, 0:PER_BANK * BD_W].rearrange(
                                           "p (s g l) -> p s g l", g=GROUPS, l=COLS)).then_inc(tri_used, 1)
                act.wait_ge(z_ready, n + 1)
                nc.scalar.copy(z_sb[:, 0, :], z_ps[:, 0:P])
                nc.scalar.activation(z_sb[:, 1, :], z_ps[:, P:2 * P], ACT.Identity,
                                     bias=b2x[:, 0:1]).then_inc(z_used, 1)
                act.wait_ge(h1_ready, n + 1)
                for m in range(TOP1 // P):
                    last = nc.scalar.activation(h1_sb[:, m, :], h1_ps[:, m * P:(m + 1) * P], ACT.Relu,
                                                bias=bt1_sb[:, m:m + 1])
                last.then_inc(h1_used, 1)
                act.wait_ge(h2_ready, n + 1)
                for m in range(TOP2 // P):
                    last = nc.scalar.activation(h2_sb[:, m, :], h2_ps[:, m * P:(m + 1) * P], ACT.Relu,
                                                bias=bt2_sb[:, m:m + 1])
                last.then_inc(h2_used, 1)
                act.wait_ge(y_ready, n + 1)
                nc.scalar.copy(y_sb[:, bass.ds(n * P, P)], y_ps[0:1, 0:P]).then_inc(y_used, 1)


def kernel(**inputs):
    import numpy as np
    import concourse.bacc as bacc
    from concourse.bass_utils import run_bass_kernel_spmd as run

    nc = bacc.Bacc("TRN2", target_bir_lowering=False, num_devices=1)
    arrays = {}

    def arg(name):
        a = np.ascontiguousarray(inputs[name])
        arrays["in_" + name] = a
        return nc.dram_tensor("in_" + name, a.shape, mybir.dt.from_np(a.dtype), kind="ExternalInput").ap()

    args = [arg("ids"), [arg(f"tbl_{f}") for f in range(FIELDS)]]
    args += [arg(name) for name in ("dense_ctx", "L0_rec_W1", "L0_rec_b1", "L0_rec_W2", "L0_rec_b2",
                                    "W_top1", "b_top1", "W_top2", "b_top2", "W_top3")]
    out = nc.dram_tensor("out_y", (BATCH, 1), mybir.dt.float32, kind="ExternalOutput").ap()
    build(nc, *args, out)
    r = run(nc, [arrays], core_ids=[0])
    return r.results[0]["out_y"]
```

```python
import concourse.bass as bass
from concourse import mybir
from contextlib import ExitStack

BATCH = 512
FIELDS = 26
EMB = 32
H = 128
DENSE = 16
TOP1, TOP2 = 512, 256

P = 128
TILES = BATCH // P
GROUPS = P // EMB
SLOTS = P // GROUPS
BANKS = 4
PER_BANK = 4
RUNS = SLOTS // PER_BANK

THIRD = FIELDS + 1
ONE = FIELDS
SPLIT = 15
LOW, HIGH = 0, 1
N_LOW, N_HIGH = SPLIT, FIELDS - SPLIT
HIGH_PAIRS = N_HIGH + 1
ROWS = [N_LOW * (N_LOW + 1) // 2, HIGH_PAIRS + N_HIGH * (N_HIGH + 1) // 2]
START = [0, ROWS[LOW], ROWS[LOW] + ROWS[HIGH]]
ONE_ONE = START[HIGH] + N_HIGH
QUAD = P // 4
STACKS = -(-N_LOW // 4)

BT1_AT = 0
BT2_AT = BT1_AT + TOP1 // P
WT3_AT = BT2_AT + TOP2 // P
B1_AT = WT3_AT + TOP2 // P
B2_AT = B1_AT + 1
VECS = B2_AT + 1


L_CHUNK = 4
L_CHUNKS = -(-FIELDS // L_CHUNK)
V_GROUPS = [(t, a, min(a + L_CHUNK, FIELDS)) for t in (LOW, HIGH) for a in range(0, FIELDS, L_CHUNK)]


def pairs_with(j):
    if j < SPLIT:
        return j * (j + 1) // 2, 0
    if j == ONE:
        return START[HIGH], SPLIT
    return START[HIGH] + HIGH_PAIRS + (j - SPLIT) * (j - SPLIT + 1) // 2, SPLIT


def build(nc, ids, tables, dense, w1, b1, w2, b2, wt1, bt1, wt2, bt2, wt3, out):
    fp32, int32 = mybir.dt.float32, mybir.dt.int32
    ALU = mybir.AluOpType
    ACT = mybir.ActivationFunctionType

    ctx = ExitStack()
    with ctx:
        def sb(name, shape, dt=fp32):
            return ctx.enter_context(nc.sbuf_tensor(name, shape, dt))

        def sem(name):
            return ctx.enter_context(nc.semaphore(name))

        idx = sb("idx", [P, TILES * FIELDS], int32)
        w1_sb = sb("w1_sb", [H, FIELDS, FIELDS])
        w2_sb = sb("w2_sb", [H, H, FIELDS])
        vec_sb = sb("vec_sb", [VECS, P])
        dense_sb = sb("dense_sb", [P, TILES, DENSE])
        wt1_sb = sb("wt1_sb", [H, 2, TOP1])
        wt1d_sb = sb("wt1d_sb", [DENSE, TOP1])
        wt2_sb = sb("wt2_sb", [P, TOP1 // P, TOP2])

        ident = sb("ident", [P, P])
        w1s = sb("w1s", [H, START[-1]])
        w1c = sb("w1c", [H, N_HIGH, N_LOW])
        w1q = sb("w1q", [H, STACKS, 4, QUAD])
        w1p = sb("w1p", [P, 2, H])
        w1x = sb("w1x", [P, STACKS, H])
        w2t = sb("w2t", [H, FIELDS, H])
        fold_t = [sb(f"fold_t{t}", [H, FIELDS, ROWS[t]]) for t in (LOW, HIGH)]
        cross = sb("cross", [H, FIELDS, N_HIGH, N_LOW])
        fold = sb("fold", [P, 2, FIELDS, H])
        b2x = sb("b2x", [H, 1])
        dense_t = sb("dense_t", [DENSE, BATCH])
        vec_t = sb("vec_t", [P, VECS])
        bt1_sb, bt2_sb = vec_t[:, BT1_AT:BT2_AT], vec_t[:, BT2_AT:WT3_AT]
        wt3_sb, b1_sb, b2_sb = vec_t[:, WT3_AT:B1_AT], vec_t[:, B1_AT:B2_AT], vec_t[:, B2_AT:VECS]

        emb = sb("emb", [P, 2, FIELDS * EMB])
        emb_t = sb("emb_t", [P, THIRD, SLOTS])
        pairs = sb("pairs", [P, START[-1], SLOTS])
        diag = sb("diag", [P, SLOTS, GROUPS, THIRD])
        triples = sb("triples", [P, 2, THIRD, P])
        stacked = sb("stacked", [P, STACKS, P])
        z_sb = sb("z_sb", [H, 2, P])
        h1_sb = sb("h1_sb", [P, TOP1 // P, P])
        h2_sb = sb("h2_sb", [P, TOP2 // P, P])
        y_sb = sb("y_sb", [1, BATCH])

        tri_ps = ctx.enter_context(nc.psum_tensor("tri_ps", [P, BANKS, 512], fp32))
        z_ps = ctx.enter_context(nc.psum_tensor("z_ps", [P, 512], fp32))
        h1_ps = ctx.enter_context(nc.psum_tensor("h1_ps", [P, 512], fp32))
        h2_ps = ctx.enter_context(nc.psum_tensor("h2_ps", [P, 512], fp32))
        y_ps = ctx.enter_context(nc.psum_tensor("y_ps", [P, 512], fp32))

        ids_in = sem("ids_in")
        w1_in = sem("w1_in")
        w2_in = sem("w2_in")
        top_in = sem("top_in")
        dense_in = sem("dense_in")
        vecs_in = sem("vecs_in")
        emb_in = [sem(f"emb_in{f}") for f in range(FIELDS)]
        ident_made = sem("ident_made")
        cleared = sem("cleared")
        halved = sem("halved")
        w1s_made = sem("w1s_made")
        w1c_made = sem("w1c_made")
        b1_put = sem("b1_put")
        trans_ps = sem("trans_ps")
        trans_used = sem("trans_used")
        fold_ps = sem("fold_ps")
        fold_used = sem("fold_used")
        added = sem("added")
        v_ps = sem("v_ps")
        v_used_act, v_used_dve = sem("v_used_act"), sem("v_used_dve")
        emb_ready = sem("emb_ready")
        diag_ready = sem("diag_ready")
        pairs_ready = sem("pairs_ready")
        tri_ready = sem("tri_ready")
        tri_used = sem("tri_used")
        zeroed = sem("zeroed")
        stack_made = sem("stack_made")
        z_ready, z_used = sem("z_ready"), sem("z_used")
        h1_ready, h1_used = sem("h1_ready"), sem("h1_used")
        h2_ready, h2_used = sem("h2_ready"), sem("h2_used")
        y_ready, y_used = sem("y_ready"), sem("y_used")
        y_out = sem("y_out")

        TRANS = L_CHUNKS + 3
        VECS_AT = 3 * P

        block = ctx.enter_context(nc.Block())

        @block.sync
        def _(sp):
            sp.dma_start(idx[:].rearrange("p (t f) -> p t f", f=FIELDS),
                         ids.rearrange("(t p) f -> p t f", p=P)).then_inc(ids_in, 16)
            sp.dma_start(w2_sb[:], w2).then_inc(w2_in, 16)
            sp.dma_start(wt2_sb[:], wt2.rearrange("(c p) n -> p c n", p=P)).then_inc(top_in, 16)
            sp.dma_start(wt1_sb[:], wt1[0:2 * H, :].rearrange("(c p) n -> p c n", p=H)).then_inc(top_in, 16)
            sp.dma_start(wt1d_sb[:], wt1[2 * H:2 * H + DENSE, :]).then_inc(top_in, 16)
            sp.wait_ge(y_used, TILES)
            sp.dma_start(out.rearrange("b x -> x b"), y_sb[:]).then_inc(y_out, 16)
            sp.wait_ge(y_out, 16)

        @block.gpsimd
        def _(pool):
            nc.gpsimd.memset(ident[:], 0.0).then_inc(ident_made, 1)
            pool.wait_ge(ident_made, 1)
            nc.gpsimd.affine_select(out=ident[:], in_=ident[:], compare_op=ALU.not_equal, fill=1.0, base=0,
                                    pattern=[[-1, P]], channel_multiplier=1).then_inc(ident_made, 1)
            pool.wait_ge(ids_in, 16)
            for t in range(TILES):
                if t >= 2:
                    pool.wait_ge(emb_ready, 2 * (t - 1))
                for f in range(FIELDS):
                    if t:
                        pool.wait_ge(emb_in[f], 16 * t)
                    col = f * EMB
                    i = t * FIELDS + f
                    nc.gpsimd.indirect_dma_start(
                        out=emb[:, t % 2, col:col + EMB], out_offset=None, in_=tables[f],
                        in_offset=bass.IndirectOffsetOnAxis(ap=idx[:, i:i + 1], axis=0)).then_inc(emb_in[f], 16)

        @block.vector
        def _(dve):
            nc.vector.memset(w1q[:], 0.0).then_inc(cleared, 1)
            nc.vector.memset(w1s[:, START[HIGH]:ONE_ONE], 0.0)
            nc.vector.memset(diag[:], 0.0).then_inc(cleared, 1)
            nc.vector.memset(emb_t[:, ONE, :], 1.0)
            nc.vector.memset(pairs[:, ONE_ONE, :], 1.0)
            nc.vector.memset(stacked[:], 0.0).then_inc(zeroed, 1)
            dve.wait_ge(cleared, 2)
            for g in range(GROUPS):
                nc.vector.memset(diag[EMB * g:EMB * (g + 1), :, g, ONE:THIRD], 1.0)

            dve.wait_ge(w1_in, 16)
            d = w1_sb[:].rearrange("h i j -> h (i j)")[:, 0:FIELDS * FIELDS:FIELDS + 1]
            nc.vector.tensor_scalar(d, d, 0.5, None, ALU.mult).then_inc(halved, 1)
            low_high, high_low = w1_sb[:, 0:SPLIT, SPLIT:FIELDS], w1_sb[:, SPLIT:FIELDS, 0:SPLIT]
            nc.vector.tensor_tensor(w1c[:], high_low, low_high.rearrange("h i c -> h c i"),
                                    ALU.add).then_inc(w1c_made, 1)
            dve.wait_ge(halved, 1)
            for j in range(FIELDS):
                at, i = pairs_with(j)
                last = nc.vector.tensor_tensor(w1s[:, at:at + j + 1 - i], w1_sb[:, i:j + 1, j],
                                               w1_sb[:, j, i:j + 1], ALU.add)
            last.then_inc(w1s_made, 1)
            dve.wait_ge(w1c_made, 1)
            for q in range(4):
                m = len(range(q, N_LOW, 4))
                last = nc.vector.tensor_copy(w1q[:, 0:m, q, 0:N_HIGH],
                                             w1c[:, :, q:N_LOW:4].rearrange("h c m -> h m c"))
            last.then_inc(w1c_made, 1)

            def spread_diag(n, first, stop):
                for g in range(GROUPS):
                    rows = slice(EMB * g, EMB * (g + 1))
                    last = nc.vector.tensor_copy(diag[rows, :, g, first:stop],
                                                 emb_t[rows, first:stop, :].rearrange("p f s -> p s f"))
                return last

            def multiply_pairs(js):
                for j in js:
                    at, i = pairs_with(j)
                    n_i = min(j, FIELDS - 1) + 1 - i
                    last = nc.vector.tensor_tensor(
                        pairs[:, at:at + n_i, :], emb_t[:, i:i + n_i, :],
                        emb_t[:, j:j + 1, :].broadcast_to([P, n_i, SLOTS]), ALU.mult)
                return last

            def multiply_tile(n):
                for t, js in ((LOW, range(0, SPLIT)), (HIGH, range(SPLIT, FIELDS))):
                    first, stop = js[0], js[-1] + 1
                    for f in js:
                        dve.wait_ge(emb_in[f], 16 * (n + 1))
                    if n and t == LOW:
                        dve.wait_ge(pairs_ready, 2 * n)
                    nc.vector.transpose(emb_t[:, first:stop, :].rearrange("p f s -> p (f s)"),
                                        emb[:, n % 2, first * EMB:stop * EMB]).then_inc(emb_ready, 1)
                    dve.wait_ge(emb_ready, 2 * n + t + 1)
                    if t == LOW:
                        if n:
                            dve.wait_ge(tri_ready, RUNS * (2 * n - 1))
                        multiply_pairs(js).then_inc(pairs_ready, 1)
                        if n:
                            dve.wait_ge(tri_ready, RUNS * 2 * n)
                        spread_diag(n, first, stop)
                    else:
                        spread_diag(n, first, stop).then_inc(diag_ready, 1)
                        multiply_pairs([ONE] + list(js)).then_inc(pairs_ready, 1)

            def hand_over(t, cols, b, rows, source):
                at, i = pairs_with(b)
                at -= START[t]
                dst = fold_t[t][:, cols, at + rows.start - i:at + rows.stop - i]
                return nc.vector.tensor_tensor(dst, dst, source, ALU.add)

            multiply_tile(0)

            low, high = slice(0, SPLIT), slice(SPLIT, FIELDS)
            dve.wait_ge(fold_used, FIELDS)
            for l in range(SPLIT):
                hand_over(LOW, high, l, slice(0, l + 1), cross[:, l, :, 0:l + 1])
            for l in range(SPLIT, FIELDS):
                last = hand_over(HIGH, low, l, slice(SPLIT, l + 1),
                                 cross[:, l, 0:l + 1 - SPLIT, :].rearrange("h c i -> h i c"))
            last.then_inc(added, 1)
            dve.wait_ge(added, 1)
            for i in range(1, SPLIT):
                last = hand_over(LOW, high, i, slice(0, i), cross[:, 0:i, :, i].rearrange("h l c -> h c l"))
            last.then_inc(added, 1)
            for c in range(SPLIT + 1, FIELDS):
                last = hand_over(HIGH, low, c, slice(SPLIT, c),
                                 cross[:, SPLIT:c, c - SPLIT, :].rearrange("h l i -> h i l"))
            last.then_inc(added, 1)
            for g in range(1, len(V_GROUPS), 2):
                t, a, b = V_GROUPS[g]
                dve.wait_ge(v_ps, g + 1)
                nc.vector.tensor_copy(fold[0:ROWS[t], t, a:b, :].rearrange("p l h -> p (l h)"),
                                      tri_ps[0:ROWS[t], g % BANKS, 0:(b - a) * H]).then_inc(v_used_dve, 1)

            for n in range(1, TILES):
                multiply_tile(n)

        @block.tensor
        def _(pe):
            def transposed(c, parts):
                if c >= BANKS:
                    pe.wait_ge(trans_used, c - BANKS + 1)
                for o, src in parts:
                    rows, cols = src.shape[1], src.shape[0]
                    last = nc.tensor.transpose(tri_ps[0:rows, c % BANKS, o:o + cols], src, ident[0:cols, 0:cols])
                last.then_inc(trans_ps, 1)

            pe.wait_ge(ident_made, 2)
            pe.wait_ge(w2_in, 16)
            for c in range(L_CHUNKS):
                ls = range(c * L_CHUNK, min(FIELDS, (c + 1) * L_CHUNK))
                parts = [((l - ls[0]) * H, w2_sb[:, :, l]) for l in ls]
                if c == L_CHUNKS - 1:
                    pe.wait_ge(vecs_in, 80)
                    parts.append((VECS_AT, vec_sb[:]))
                transposed(c, parts)
            pe.wait_ge(dense_in, 16)
            transposed(L_CHUNKS, [(t * P, dense_sb[:, t, :]) for t in range(TILES)])
            pe.wait_ge(w1s_made, 1)
            pe.wait_ge(b1_put, 3)
            transposed(L_CHUNKS + 1, [(t * H, w1s[:, START[t]:START[t + 1]]) for t in (LOW, HIGH)])
            pe.wait_ge(w1c_made, 2)
            transposed(L_CHUNKS + 2, [(m * H, w1q[:, m, :, :].rearrange("h q c -> h (q c)")) for m in range(STACKS)])

            pe.wait_ge(trans_used, L_CHUNKS)
            for l in range(FIELDS):
                c = TRANS + l
                if l < BANKS:
                    pe.wait_ge(trans_used, c - BANKS + 1)
                else:
                    pe.wait_ge(fold_used, l - BANKS + 1)
                nc.tensor.matmul(tri_ps[:, c % BANKS, 0:START[-1]], w2t[:, l, :], w1s[:], start=True, stop=True)
                last = nc.tensor.matmul(tri_ps[:, c % BANKS, START[-1]:START[-1] + N_HIGH * N_LOW], w2t[:, l, :],
                                        w1c[:].rearrange("h c i -> h (c i)"), start=True, stop=True)
                last.then_inc(fold_ps, 1)
            pe.wait_ge(fold_used, FIELDS)

            def make_triples(n, t):
                pe.wait_ge(pairs_ready, n * 2 + (t + 1))
                if t == LOW:
                    pe.wait_ge(diag_ready, n + 1)
                width = GROUPS * THIRD
                for r in range(RUNS):
                    run = t * RUNS + r
                    if not (type(n) is int and run < BANKS):
                        pe.wait_ge(tri_used, n * (2 * RUNS) + (run - BANKS + 1))
                    for q in range(PER_BANK):
                        s = r * PER_BANK + q
                        last = nc.tensor.matmul(
                            tri_ps[0:ROWS[t], run % BANKS, q * width:(q + 1) * width],
                            pairs[:, START[t]:START[t + 1], s],
                            diag[:, s, :, :].rearrange("p g l -> p (g l)"), start=True, stop=True)
                    last.then_inc(tri_ready, 1)

            def make_z(n):
                for t in (LOW, HIGH):
                    pe.wait_ge(tri_used, n * (2 * RUNS) + RUNS * (t + 1))
                    for l in range(FIELDS):
                        nc.tensor.matmul(z_ps[:, P:2 * P], fold[0:ROWS[t], t, l, :], triples[0:ROWS[t], t, l, :],
                                         start=(t == LOW and l == 0), stop=(t == HIGH and l == FIELDS - 1))
                for t in (LOW, HIGH):
                    nc.tensor.matmul(z_ps[:, 0:P], w1p[0:ROWS[t], t, :], triples[0:ROWS[t], t, ONE, :],
                                     start=(t == LOW), stop=False)
                pe.wait_ge(stack_made, n + 1)
                for m in range(STACKS):
                    last = nc.tensor.matmul(z_ps[:, 0:P], w1x[:, m, :], stacked[:, m, :],
                                            start=False, stop=(m == STACKS - 1))
                last.then_inc(z_ready, 1)

            def layer1(n):
                pe.wait_ge(z_used, n + 1)
                dense_n = dense_t[:, n * P:(n + 1) * P] if type(n) is int else dense_t[:, bass.ds(n * P, P)]
                for m in range(TOP1 // P):
                    cols = slice(m * P, (m + 1) * P)
                    nc.tensor.matmul(h1_ps[:, cols], wt1d_sb[:, cols], dense_n, start=True, stop=False)
                    for c in range(2):
                        last = nc.tensor.matmul(h1_ps[:, cols], wt1_sb[:, c, cols], z_sb[:, c, :],
                                                start=False, stop=(c == 1))
                last.then_inc(h1_ready, 1)

            def layer2(n):
                pe.wait_ge(h1_used, n + 1)
                for m in range(TOP2 // P):
                    cols = slice(m * P, (m + 1) * P)
                    for c in range(TOP1 // P):
                        last = nc.tensor.matmul(h2_ps[:, cols], wt2_sb[:, c, cols], h1_sb[:, c, :],
                                                start=(c == 0), stop=(c == TOP1 // P - 1))
                last.then_inc(h2_ready, 1)

            def layer3(n):
                pe.wait_ge(h2_used, n + 1)
                for c in range(TOP2 // P):
                    last = nc.tensor.matmul(y_ps[0:1, 0:P], wt3_sb[:, c:c + 1], h2_sb[:, c, :],
                                            start=(c == 0), stop=(c == TOP2 // P - 1))
                last.then_inc(y_ready, 1)

            make_triples(0, LOW)
            make_triples(0, HIGH)

            pe.wait_ge(added, 2)
            for g, (t, a, b) in enumerate(V_GROUPS):
                if g < BANKS:
                    pe.wait_ge(tri_used, 2 * RUNS - BANKS + g + 1)
                else:
                    used = (v_used_act, v_used_dve)[g % 2]
                    pe.wait_ge(used, g // 2 - 1)
                if t == HIGH:
                    pe.wait_ge(added, 3)
                for l in range(a, b):
                    last = nc.tensor.transpose(tri_ps[0:ROWS[t], g % BANKS, (l - a) * H:(l - a + 1) * H],
                                               fold_t[t][:, l, :], ident[:])
                last.then_inc(v_ps, 1)
            pe.wait_ge(v_used_act, len(V_GROUPS) // 2)
            pe.wait_ge(v_used_dve, len(V_GROUPS) // 2)
            pe.wait_ge(top_in, 48)

            with pe.Fori(0, TILES - 1) as n:
                make_z(n)
                make_triples(n + 1, LOW)
                layer1(n)
                make_triples(n + 1, HIGH)
                layer2(n)
                layer3(n)
            make_z(TILES - 1)
            layer1(TILES - 1)
            layer2(TILES - 1)
            layer3(TILES - 1)

        @block.scalar
        def _(act):
            act.dma_start(w1_sb[:], w1).then_inc(w1_in, 16)
            for at, v in ((BT1_AT, bt1), (BT2_AT, bt2), (WT3_AT, wt3.rearrange("n o -> (n o)")), (B1_AT, b1), (B2_AT, b2)):
                rows = v.shape[0] // P
                act.dma_start(vec_sb[at:at + rows, :], v.rearrange("(c p) -> c p", p=P)).then_inc(vecs_in, 16)
            act.dma_start(dense_sb[:], dense.rearrange("(t p) d -> p t d", p=P)).then_inc(dense_in, 16)

            for c in range(L_CHUNKS):
                ls = slice(c * L_CHUNK, min(FIELDS, (c + 1) * L_CHUNK))
                act.wait_ge(trans_ps, c + 1)
                if c == L_CHUNKS - 1:
                    vecs = tri_ps[:, c % BANKS, VECS_AT:VECS_AT + VECS]
                    nc.scalar.copy(vec_t[:], vecs).then_inc(b1_put, 1)
                    nc.scalar.copy(w1s[:, ONE_ONE:ONE_ONE + 1], vecs[:, B1_AT:B2_AT]).then_inc(b1_put, 1)
                    nc.scalar.mul(b2x[:], vecs[:, B2_AT:VECS], float(EMB)).then_inc(b1_put, 1)
                nc.scalar.copy(w2t[:, ls, :].rearrange("p l h -> p (l h)"),
                               tri_ps[:, c % BANKS, 0:(ls.stop - ls.start) * H]).then_inc(trans_used, 1)
            c = L_CHUNKS
            act.wait_ge(trans_ps, c + 1)
            nc.scalar.copy(dense_t[:], tri_ps[0:DENSE, c % BANKS, 0:BATCH]).then_inc(trans_used, 1)
            c = L_CHUNKS + 1
            act.wait_ge(trans_ps, c + 1)
            for t in (LOW, HIGH):
                last = nc.scalar.copy(w1p[0:ROWS[t], t, :], tri_ps[0:ROWS[t], c % BANKS, t * H:(t + 1) * H])
            last.then_inc(trans_used, 1)
            c = L_CHUNKS + 2
            act.wait_ge(trans_ps, c + 1)
            nc.scalar.copy(w1x[:].rearrange("p m h -> p (m h)"), tri_ps[:, c % BANKS, 0:STACKS * H]).then_inc(trans_used, 1)

            for l in range(FIELDS):
                bank = tri_ps[:, (TRANS + l) % BANKS, :]
                act.wait_ge(fold_ps, l + 1)
                for t in (LOW, HIGH):
                    nc.scalar.copy(fold_t[t][:, l, :], bank[:, START[t]:START[t + 1]])
                nc.scalar.copy(cross[:, l, :, :].rearrange("h c i -> h (c i)"),
                               bank[:, START[-1]:START[-1] + N_HIGH * N_LOW]).then_inc(fold_used, 1)

            def copy_triples(n, t):
                dst = triples[0:ROWS[t], t, :, :].rearrange("p l (g s) -> p s g l", g=GROUPS)
                for r in range(RUNS):
                    run = t * RUNS + r
                    act.wait_ge(tri_ready, n * (2 * RUNS) + (run + 1))
                    nc.scalar.copy(dst[:, r * PER_BANK:(r + 1) * PER_BANK, :, :],
                                   tri_ps[0:ROWS[t], run % BANKS, 0:PER_BANK * GROUPS * THIRD].rearrange(
                                       "p (s g l) -> p s g l", g=GROUPS, l=THIRD)).then_inc(tri_used, 1)

            def stack(n):
                act.wait_ge(tri_used, n * (2 * RUNS) + 2 * RUNS)
                for q in range(4):
                    m = len(range(q, N_LOW, 4))
                    last = nc.scalar.copy(stacked[QUAD * q:QUAD * q + N_HIGH, 0:m, :],
                                          triples[0:N_HIGH, HIGH, q:N_LOW:4, :])
                last.then_inc(stack_made, 1)

            def copy_z(n):
                act.wait_ge(z_ready, n + 1)
                nc.scalar.copy(z_sb[:, 0, :], z_ps[:, 0:P])
                nc.scalar.activation(z_sb[:, 1, :], z_ps[:, P:2 * P], ACT.Identity,
                                     bias=b2x[:, 0:1]).then_inc(z_used, 1)

            def hidden1(n):
                act.wait_ge(h1_ready, n + 1)
                for m in range(TOP1 // P):
                    last = nc.scalar.activation(h1_sb[:, m, :], h1_ps[:, m * P:(m + 1) * P], ACT.Relu,
                                                bias=bt1_sb[:, m:m + 1])
                last.then_inc(h1_used, 1)

            def hidden2(n):
                act.wait_ge(h2_ready, n + 1)
                for m in range(TOP2 // P):
                    last = nc.scalar.activation(h2_sb[:, m, :], h2_ps[:, m * P:(m + 1) * P], ACT.Relu,
                                                bias=bt2_sb[:, m:m + 1])
                last.then_inc(h2_used, 1)

            def copy_y(n):
                act.wait_ge(y_ready, n + 1)
                y_n = y_sb[:, n * P:(n + 1) * P] if type(n) is int else y_sb[:, bass.ds(n * P, P)]
                nc.scalar.copy(y_n, y_ps[0:1, 0:P]).then_inc(y_used, 1)

            copy_triples(0, LOW)
            copy_triples(0, HIGH)
            act.wait_ge(zeroed, 1)
            stack(0)
            for g in range(0, len(V_GROUPS), 2):
                t, a, b = V_GROUPS[g]
                act.wait_ge(v_ps, g + 1)
                nc.scalar.copy(fold[0:ROWS[t], t, a:b, :].rearrange("p l h -> p (l h)"),
                               tri_ps[0:ROWS[t], g % BANKS, 0:(b - a) * H]).then_inc(v_used_act, 1)

            with act.Fori(0, TILES - 1) as n:
                copy_z(n)
                copy_triples(n + 1, LOW)
                hidden1(n)
                copy_triples(n + 1, HIGH)
                stack(n + 1)
                hidden2(n)
                copy_y(n)
            copy_z(TILES - 1)
            hidden1(TILES - 1)
            hidden2(TILES - 1)
            copy_y(TILES - 1)


def kernel(**inputs):
    import numpy as np
    import concourse.bacc as bacc
    from concourse.bass_utils import run_bass_kernel_spmd as run

    nc = bacc.Bacc("TRN2", target_bir_lowering=False, num_devices=1)
    arrays = {}

    def arg(name):
        a = np.ascontiguousarray(inputs[name])
        arrays["in_" + name] = a
        return nc.dram_tensor("in_" + name, a.shape, mybir.dt.from_np(a.dtype), kind="ExternalInput").ap()

    args = [arg("ids"), [arg(f"tbl_{f}") for f in range(FIELDS)]]
    args += [arg(name) for name in ("dense_ctx", "L0_rec_W1", "L0_rec_b1", "L0_rec_W2", "L0_rec_b2",
                                    "W_top1", "b_top1", "W_top2", "b_top2", "W_top3")]
    out = nc.dram_tensor("out_y", (BATCH, 1), mybir.dt.float32, kind="ExternalOutput").ap()
    build(nc, *args, out)
    r = run(nc, [arrays], core_ids=[0])
    return r.results[0]["out_y"]
```

```python
import concourse.bass as bass
from concourse import mybir
from contextlib import ExitStack

BATCH = 512
FIELDS = 26
EMB = 32
H = 128
DENSE = 16
TOP1, TOP2 = 512, 256

P = 128
TILES = BATCH // P
GROUPS = P // EMB
SLOTS = P // GROUPS
BANKS = 4
PER_BANK = 4
RUNS = SLOTS // PER_BANK

THIRD = FIELDS + 1
ONE = FIELDS
SPLIT = 14
BASE = 5
LOW, HIGH = 0, 1
FROM = [BASE, 0]
N_LOW, N_HIGH = SPLIT, FIELDS - SPLIT
HIGH_PAIRS = N_HIGH + 1
BASE_ROWS = BASE * (BASE + 1) // 2
SUMMED = [N_LOW * (N_LOW + 1) // 2, HIGH_PAIRS + N_HIGH * (N_HIGH + 1) // 2]
MIDDLE = 3
MID_STOP = SPLIT + MIDDLE
MIDDLE_ROWS = 1 + MIDDLE * (MIDDLE + 1) // 2
N_ABOVE = FIELDS - MID_STOP
ROWS = [SUMMED[LOW] + MIDDLE_ROWS, SUMMED[HIGH] + BASE_ROWS]
THIRDS = [range(BASE, FIELDS), [l for l in range(FIELDS) if not SPLIT <= l < MID_STOP]]
START = [0, ROWS[LOW], ROWS[LOW] + ROWS[HIGH]]
ONE_ONE = START[HIGH] + N_HIGH
W1_AT = [SUMMED[HIGH], 0]
FOLDED_HIGH = SUMMED[HIGH] - N_HIGH
QUAD = P // 4
STACKS = -(-N_LOW // 4)

BT1_AT = 0
BT2_AT = BT1_AT + TOP1 // P
WT3_AT = BT2_AT + TOP2 // P
B1_AT = WT3_AT + TOP2 // P
B2_AT = B1_AT + 1
VECS = B2_AT + 1

W2_PIECES = [(SPLIT, FIELDS), (BASE, SPLIT), (0, BASE)]
EARLY, MOST = 4, 12


def groups(first, stop):
    return [(a, min(a + 4, stop)) for a in range(first, stop, 4)]


LOW_GROUPS = groups(BASE, SPLIT) + groups(SPLIT, FIELDS)
LOWEST_GROUPS = len(groups(BASE, SPLIT))
HIGH_GROUPS = groups(0, SPLIT)
EARLY_GROUPS = groups(MID_STOP, FIELDS)
LATE = 23
PARTS = [(0, SPLIT), (SPLIT, LATE), (LATE, FIELDS)]


def pairs_with(j):
    if j < SPLIT:
        return j * (j + 1) // 2, 0
    if j == ONE:
        return START[HIGH], SPLIT
    return START[HIGH] + HIGH_PAIRS + (j - SPLIT) * (j - SPLIT + 1) // 2, SPLIT


def build(nc, ids, tables, vecs, dense, w1, w2, wt1, wt2, out):
    fp32, int32 = mybir.dt.float32, mybir.dt.int32
    ALU = mybir.AluOpType
    ACT = mybir.ActivationFunctionType

    ctx = ExitStack()
    with ctx:
        def sb(name, shape, dt=fp32):
            return ctx.enter_context(nc.sbuf_tensor(name, shape, dt))

        def sem(name):
            return ctx.enter_context(nc.semaphore(name))

        idx = sb("idx", [P, TILES * FIELDS], int32)
        w1_sb = sb("w1_sb", [H, FIELDS, FIELDS])
        w2_sb = sb("w2_sb", [H, FIELDS, H])
        vec_sb = sb("vec_sb", [P, VECS])
        bt1_sb, bt2_sb = vec_sb[:, BT1_AT:BT2_AT], vec_sb[:, BT2_AT:WT3_AT]
        wt3_sb, b1_sb, b2_sb = vec_sb[:, WT3_AT:B1_AT], vec_sb[:, B1_AT:B2_AT], vec_sb[:, B2_AT:VECS]
        dense_sb = sb("dense_sb", [DENSE, BATCH])
        wt1_sb = sb("wt1_sb", [H, 2, TOP1])
        wt1d_sb = sb("wt1d_sb", [DENSE, TOP1])
        wt2_sb = sb("wt2_sb", [P, TOP1 // P, TOP2])

        ident = sb("ident", [P, P])
        w1s = sb("w1s", [H, sum(SUMMED)])
        w1c = sb("w1c", [H, N_HIGH, N_LOW])
        w1b = sb("w1b", [H, N_LOW - BASE, N_LOW])
        w1m = sb("w1m", [H, MIDDLE, N_ABOVE])
        w1q = sb("w1q", [H, STACKS, 4, QUAD])
        w1p = sb("w1p", [P, 2, H])
        w1x = sb("w1x", [P, STACKS, H])
        fold_t = [sb(f"fold_t{t}", [H, FIELDS - FROM[t], ROWS[t]]) for t in (LOW, HIGH)]
        cross = sb("cross", [H, FIELDS, N_HIGH, N_LOW])
        below = sb("below", [H, BASE, N_LOW - BASE, N_LOW])
        middle = sb("middle", [H, MIDDLE, MIDDLE, N_ABOVE])
        fold = sb("fold", [P, 2, FIELDS, H])
        b2x = sb("b2x", [H, 1])

        dense_h1 = sb("dense_h1", [P, TOP1 // P, (TILES - 1) * P])

        emb = sb("emb", [P, 2, FIELDS * EMB])
        emb_t = sb("emb_t", [P, THIRD, SLOTS])
        pairs = sb("pairs", [P, START[-1], SLOTS])
        diag = sb("diag", [P, SLOTS, GROUPS, THIRD])
        triples = sb("triples", [P, 2, THIRD, P])
        stacked = sb("stacked", [P, STACKS, P])
        z_sb = sb("z_sb", [H, 2, P])
        h1_sum = sb("h1_sum", [P, TOP1 // P, P])
        h1_sb = sb("h1_sb", [P, TOP1 // P, P])
        h2_sb = sb("h2_sb", [P, TOP2 // P, P])
        y_sb = sb("y_sb", [1, BATCH])

        tri_ps = ctx.enter_context(nc.psum_tensor("tri_ps", [P, BANKS, 512], fp32))
        z_ps = ctx.enter_context(nc.psum_tensor("z_ps", [P, 512], fp32))
        h1_ps = ctx.enter_context(nc.psum_tensor("h1_ps", [P, 512], fp32))
        h2_ps = ctx.enter_context(nc.psum_tensor("h2_ps", [P, 512], fp32))
        y_ps = ctx.enter_context(nc.psum_tensor("y_ps", [P, 512], fp32))

        ids_in = sem("ids_in")
        w1_in = sem("w1_in")
        w2_in = [sem(f"w2_in{i}") for i in range(len(W2_PIECES))]
        top_in = sem("top_in")
        dense_in = sem("dense_in")
        dense_w_in = sem("dense_w_in")
        vecs_in = sem("vecs_in")
        emb_in = [sem(f"emb_in{f}") for f in range(FIELDS)]
        ident_made = sem("ident_made")
        cleared = sem("cleared")
        halved = sem("halved")
        w1s_made = sem("w1s_made")
        w1c_made = sem("w1c_made")
        biases_made = sem("biases_made")
        w1_ps = sem("w1_ps")
        w1_used = sem("w1_used")
        fold_ps = sem("fold_ps")
        fold_used = sem("fold_used")
        added = sem("added")
        early_ps, early_used = sem("early_ps"), sem("early_used")
        low_ps, low_used = sem("low_ps"), sem("low_used")
        high_ps, high_used = sem("high_ps"), sem("high_used")
        emb_ready = sem("emb_ready")
        diag_ready = sem("diag_ready")
        diag_shared = sem("diag_shared")
        pairs_ready = sem("pairs_ready")
        tri_ready = sem("tri_ready")
        tri_used = sem("tri_used")
        zeroed = sem("zeroed")
        stack_made = sem("stack_made")
        z_ready, z_used = sem("z_ready"), sem("z_used")
        dense_ready, dense_used = sem("dense_ready"), sem("dense_used")
        h1_summed = sem("h1_summed")
        h1_ready, h1_used = sem("h1_ready"), sem("h1_used")
        h2_ready, h2_used = sem("h2_ready"), sem("h2_used")
        h1_used_dve, h2_used_dve = sem("h1_used_dve"), sem("h2_used_dve")
        y_ready, y_used = sem("y_ready"), sem("y_used")
        y_out = sem("y_out")

        z1_ps = h2_ps[:, TOP2:TOP2 + P]
        h1_dve_ps, h2_dve_ps = tri_ps[:, 0, :], tri_ps[:, 1, :]
        tower_ps = [z_ps, h1_ps, h2_ps, y_ps]
        WARM_UP = 16
        W1S_BANK, W1Q_BANK = range(2)
        FOLD_BANK = 2
        FOLD_ORDER = [l for first, stop in W2_PIECES for l in range(first, stop)]
        MIDDLE_ADDED, LOWEST_ADDED, LOW_ADDED, HIGH_ADDED = 2, 5, 6, 8
        BY_DVE = 3
        w1c_row, w1b_row, w1m_row = (w.rearrange("h c i -> h (c i)") for w in (w1c[:], w1b[:], w1m[:]))
        LOW_AT = FOLDED_HIGH
        CROSS_AT = LOW_AT + SUMMED[LOW]
        BELOW_AT = CROSS_AT + N_HIGH * N_LOW

        def parts_of(l):
            parts = [(0, w1s[:, N_HIGH:sum(SUMMED)]), (CROSS_AT, w1c_row)]
            if l < BASE:
                parts += [(BELOW_AT, w1b_row)]
            if SPLIT <= l < MID_STOP:
                parts += [(BELOW_AT, w1m_row)]
            return parts

        def spread_diag(copy, spread_groups, first, stop):
            for g in spread_groups:
                rows = slice(EMB * g, EMB * (g + 1))
                last = copy(diag[rows, :, g, first:stop], emb_t[rows, first:stop, :].rearrange("p f s -> p s f"))
            return last

        block = ctx.enter_context(nc.Block())

        @block.sync
        def _(sp):
            sp.dma_start(idx[:].rearrange("p (t f) -> p t f", f=FIELDS),
                         ids.rearrange("(t p) f -> p t f", p=P)).then_inc(ids_in, 16)
            sp.dma_start(w1_sb[:], w1).then_inc(w1_in, 16)
            for i, (first, stop) in enumerate(W2_PIECES):
                sp.dma_start(w2_sb[:, first:stop, :], w2[:, first:stop, :]).then_inc(w2_in[i], 16)
            sp.dma_start(wt2_sb[:], wt2.rearrange("(c p) n -> p c n", p=P)).then_inc(top_in, 16)
            sp.dma_start(wt1_sb[:], wt1[0:2 * H, :].rearrange("(c p) n -> p c n", p=H)).then_inc(top_in, 16)
            sp.wait_ge(y_used, TILES)
            sp.dma_start(out.rearrange("b x -> x b"), y_sb[:]).then_inc(y_out, 16)
            sp.wait_ge(y_out, 16)

        @block.gpsimd
        def _(pool):
            nc.gpsimd.memset(ident[:], 0.0).then_inc(ident_made, 1)
            pool.wait_ge(ident_made, 1)
            nc.gpsimd.affine_select(out=ident[:], in_=ident[:], compare_op=ALU.not_equal, fill=1.0, base=0,
                                    pattern=[[-1, P]], channel_multiplier=1).then_inc(ident_made, 1)
            pool.dma_start(vec_sb[:], vecs).then_inc(vecs_in, 16)
            pool.wait_ge(ids_in, 16)
            for t in range(TILES):
                if t >= 2:
                    pool.wait_ge(emb_ready, len(PARTS) * (t - 1))
                for f in range(FIELDS):
                    if t:
                        pool.wait_ge(emb_in[f], 16 * t)
                    col = f * EMB
                    i = t * FIELDS + f
                    nc.gpsimd.indirect_dma_start(
                        out=emb[:, t % 2, col:col + EMB], out_offset=None, in_=tables[f],
                        in_offset=bass.IndirectOffsetOnAxis(ap=idx[:, i:i + 1], axis=0)).then_inc(emb_in[f], 16)

        @block.vector
        def _(dve):
            nc.vector.memset(w1q[:], 0.0).then_inc(cleared, 1)
            nc.vector.memset(w1s[:, W1_AT[HIGH]:W1_AT[HIGH] + N_HIGH], 0.0)

            dve.wait_ge(w1_in, 16)
            d = w1_sb[:].rearrange("h i j -> h (i j)")[:, 0:FIELDS * FIELDS:FIELDS + 1]
            nc.vector.tensor_scalar(d, d, 0.5, None, ALU.mult).then_inc(halved, 1)
            low_high, high_low = w1_sb[:, 0:SPLIT, SPLIT:FIELDS], w1_sb[:, SPLIT:FIELDS, 0:SPLIT]
            nc.vector.tensor_tensor(w1c[:], high_low, low_high.rearrange("h i c -> h c i"),
                                    ALU.add).then_inc(w1c_made, 1)
            dve.wait_ge(halved, 1)
            nc.vector.tensor_tensor(w1b[:], w1_sb[:, BASE:SPLIT, 0:SPLIT],
                                    w1_sb[:, 0:SPLIT, BASE:SPLIT].rearrange("h i j -> h j i"), ALU.add)
            nc.vector.tensor_tensor(w1m[:], w1_sb[:, SPLIT:MID_STOP, MID_STOP:FIELDS],
                                    w1_sb[:, MID_STOP:FIELDS, SPLIT:MID_STOP].rearrange("h i j -> h j i"), ALU.add)
            for j in range(FIELDS):
                at, i = pairs_with(j)
                t = LOW if j < SPLIT else HIGH
                at += W1_AT[t] - START[t]
                last = nc.vector.tensor_tensor(w1s[:, at:at + j + 1 - i], w1_sb[:, i:j + 1, j],
                                               w1_sb[:, j, i:j + 1], ALU.add)
            last.then_inc(w1s_made, 1)
            dve.wait_ge(w1c_made, 1)
            dve.wait_ge(cleared, 1)
            for q in range(4):
                m = len(range(q, N_LOW, 4))
                last = nc.vector.tensor_copy(w1q[:, 0:m, q, 0:N_HIGH],
                                             w1c[:, :, q:N_LOW:4].rearrange("h c m -> h m c"))
            last.then_inc(w1c_made, 1)

            nc.vector.memset(diag[:], 0.0).then_inc(cleared, 1)
            dve.wait_ge(cleared, 2)
            for g in range(GROUPS):
                nc.vector.memset(diag[EMB * g:EMB * (g + 1), :, g, ONE:THIRD], 1.0)
            nc.vector.memset(emb_t[:, ONE, :], 1.0)
            nc.vector.memset(pairs[:, ONE_ONE, :], 1.0)
            nc.vector.memset(pairs[:, SUMMED[LOW], :], 1.0)
            for cols in (slice(0, SPLIT - BASE), slice(MID_STOP - BASE, FIELDS - BASE)):
                nc.vector.memset(fold_t[LOW][:, cols, SUMMED[LOW]:ROWS[LOW]], 0.0)
            nc.vector.memset(fold_t[HIGH][:, BASE:FIELDS, SUMMED[HIGH]:ROWS[HIGH]], 0.0)
            nc.vector.memset(fold_t[HIGH][:, :, 0:N_HIGH], 0.0)
            nc.vector.memset(stacked[:], 0.0).then_inc(zeroed, 1)

            def multiply_pairs(js):
                for j in js:
                    at, i = pairs_with(j)
                    n_i = min(j, FIELDS - 1) + 1 - i
                    last = nc.vector.tensor_tensor(
                        pairs[:, at:at + n_i, :], emb_t[:, i:i + n_i, :],
                        emb_t[:, j:j + 1, :].broadcast_to([P, n_i, SLOTS]), ALU.mult)
                return last

            def multiply_base():
                at = START[HIGH] + SUMMED[HIGH] - pairs_with(0)[0]
                for j in range(BASE):
                    row = at + pairs_with(j)[0]
                    nc.vector.tensor_tensor(pairs[:, row:row + j + 1, :], emb_t[:, 0:j + 1, :],
                                            emb_t[:, j:j + 1, :].broadcast_to([P, j + 1, SLOTS]), ALU.mult)

            def multiply_middle():
                at = SUMMED[LOW] + 1 - pairs_with(SPLIT)[0]
                for j in range(SPLIT, MID_STOP):
                    row, n_i = at + pairs_with(j)[0], j + 1 - SPLIT
                    nc.vector.tensor_tensor(pairs[:, row:row + n_i, :], emb_t[:, SPLIT:j + 1, :],
                                            emb_t[:, j:j + 1, :].broadcast_to([P, n_i, SLOTS]), ALU.mult)

            def place_fields(n, part, and_diag=True):
                first, stop = PARTS[part]
                for f in range(first, stop):
                    dve.wait_ge(emb_in[f], 16 * (n + 1))
                nc.vector.transpose(emb_t[:, first:stop, :].rearrange("p f s -> p (f s)"),
                                    emb[:, n % 2, first * EMB:stop * EMB]).then_inc(emb_ready, 1)
                dve.wait_ge(emb_ready, len(PARTS) * n + part + 1)
                if and_diag:
                    return spread_diag(nc.vector.tensor_copy, range(GROUPS if n else BY_DVE), first, stop)

            def multiply_low(n):
                if n:
                    dve.wait_ge(pairs_ready, 2 * n)
                if n == 1:
                    dve.wait_ge(diag_shared, 1)
                place_fields(n, 0, and_diag=False)
                if n:
                    dve.wait_ge(tri_ready, RUNS * (2 * n - 1))
                multiply_pairs(range(0, SPLIT)).then_inc(pairs_ready, 1)
                if n:
                    dve.wait_ge(tri_ready, RUNS * 2 * n)
                if n:
                    spread_diag(nc.vector.tensor_copy, range(GROUPS), 0, SPLIT)

            def multiply_high(n):
                if n:
                    place_fields(n, 1)
                    multiply_middle()
                place_fields(n, 2).then_inc(diag_ready, 1)
                multiply_base()
                multiply_pairs([ONE] + list(range(SPLIT, FIELDS))).then_inc(pairs_ready, 1)

            def hand_over(t, cols, b, rows, source):
                at, i = pairs_with(b)
                at -= START[t]
                cols = slice(cols.start - FROM[t], cols.stop - FROM[t])
                dst = fold_t[t][:, cols, at + rows.start - i:at + rows.stop - i]
                return nc.vector.tensor_tensor(dst, dst, source, ALU.add)

            low, high = slice(0, SPLIT), slice(SPLIT, FIELDS)

            def cross_as_higher(ls):
                for l in ls:
                    last = hand_over(LOW, high, l, slice(0, l + 1), cross[:, l, :, 0:l + 1])
                return last

            def cross_as_lower(fields):
                for i in fields:
                    last = hand_over(LOW, high, i, slice(0, i), cross[:, 0:i, :, i].rearrange("h l c -> h c l"))
                return last

            dve.wait_ge(fold_used, N_HIGH)
            for l in range(SPLIT, MID_STOP):
                for c2 in range(MID_STOP, FIELDS):
                    at = pairs_with(c2)[0] - START[HIGH]
                    dst = fold_t[HIGH][:, MID_STOP:c2 + 1, at + l - SPLIT]
                    nc.vector.tensor_tensor(dst, dst, fold_t[HIGH][:, l, at + MIDDLE:at + c2 + 1 - SPLIT], ALU.add)
            for turn in range(2):
                if turn:
                    dve.wait_ge(added, 1)
                for l in range(MIDDLE):
                    for c in range(MIDDLE):
                        if (l > c) == turn:
                            row = pairs_with(SPLIT + max(l, c))[0] - START[HIGH] + min(l, c)
                            dst = fold_t[HIGH][:, MID_STOP:FIELDS, row]
                            last = nc.vector.tensor_tensor(dst, dst, middle[:, l, c, :], ALU.add)
                last.then_inc(added, 1)
            low_order = FOLD_ORDER[N_HIGH:FIELDS]
            dve.wait_ge(fold_used, N_HIGH + EARLY)
            cross_as_higher(low_order[:EARLY]).then_inc(added, 1)
            multiply_low(0)
            dve.wait_ge(fold_used, N_HIGH + MOST)
            cross_as_higher(low_order[EARLY:MOST])
            dve.wait_ge(fold_used, FIELDS)
            cross_as_higher(low_order[MOST:])
            for l in range(BASE):
                last = hand_over(LOW, slice(BASE, SPLIT), l, slice(0, l + 1), below[:, l, :, 0:l + 1])
            last.then_inc(added, 1)
            dve.wait_ge(added, 4)
            for i in range(1, SPLIT):
                a, j = slice(0, min(i, BASE)), slice(max(i, BASE), SPLIT)
                last = hand_over(LOW, j, i, a, below[:, a, j.start - BASE:N_LOW - BASE, i].rearrange("h l j -> h j l"))
            last.then_inc(added, 1)
            place_fields(0, 1)
            multiply_middle()
            cross_as_lower(range(1, SPLIT)).then_inc(added, 1)
            multiply_high(0)
            for l in range(SPLIT, FIELDS):
                last = hand_over(HIGH, low, l, slice(SPLIT, l + 1),
                                 cross[:, l, 0:l + 1 - SPLIT, :].rearrange("h c i -> h i c"))
            last.then_inc(added, 1)
            dve.wait_ge(added, 7)
            for c in range(SPLIT + 1, FIELDS):
                last = hand_over(HIGH, low, c, slice(SPLIT, c),
                                 cross[:, SPLIT:c, c - SPLIT, :].rearrange("h l i -> h i l"))
            last.then_inc(added, 1)
            for g, (a, b) in enumerate(HIGH_GROUPS):
                dve.wait_ge(high_ps, g + 1)
                nc.vector.tensor_copy(fold[0:ROWS[HIGH], HIGH, a:b, :].rearrange("p l h -> p (l h)"),
                                      tower_ps[g][0:ROWS[HIGH], 0:(b - a) * H]).then_inc(high_used, 1)

            def add_dense(n):
                dve.wait_ge(h1_ready, n + 1)
                if n:
                    dve.wait_ge(h1_used, n)
                nc.vector.tensor_tensor(h1_sum[:], h1_ps[:].rearrange("p (m r) -> p m r", r=P),
                                        dense_h1[:, :, n * P:(n + 1) * P], ALU.add).then_inc(h1_summed, 1)

            dve.wait_ge(dense_used, TOP1 // P)
            for n in range(1, TILES):
                multiply_low(n)
                multiply_high(n)
                add_dense(n - 1)

            dve.wait_ge(h1_ready, TILES)
            dve.wait_ge(vecs_in, 16)
            for m in range(TOP1 // P // 2, TOP1 // P):
                nc.vector.tensor_scalar(h1_sb[:, m, :], h1_dve_ps[:, m * P:(m + 1) * P], bt1_sb[:, m:m + 1], 0.0,
                                        ALU.add, ALU.max).then_inc(h1_used_dve, 1)
            dve.wait_ge(h2_ready, TILES)
            for m in range(TOP2 // P // 2, TOP2 // P):
                last = nc.vector.tensor_scalar(h2_sb[:, m, :], h2_dve_ps[:, m * P:(m + 1) * P], bt2_sb[:, m:m + 1], 0.0,
                                               ALU.add, ALU.max)
            last.then_inc(h2_used_dve, 1)

        @block.tensor
        def _(pe):
            def keep_warm(matmuls):
                for _ in range(matmuls):
                    nc.tensor.matmul(y_ps[:, 0:P], ident[:], ident[:], start=True, stop=True)

            def transpose_w1(bank, parts):
                for i, weights in enumerate(parts):
                    cols = weights.shape[1]
                    last = nc.tensor.transpose(tri_ps[0:cols, bank, i * H:(i + 1) * H], weights, ident[:])
                last.then_inc(w1_ps, 1)

            pe.wait_ge(ident_made, 2)
            keep_warm(WARM_UP)
            pe.wait_ge(w1s_made, 1)
            pe.wait_ge(biases_made, 1)
            transpose_w1(W1S_BANK, [w1s[:, W1_AT[t]:W1_AT[t] + SUMMED[t]] for t in (LOW, HIGH)])
            pe.wait_ge(w1c_made, 2)
            transpose_w1(W1Q_BANK, [w1q[:, m, :, :].rearrange("h q c -> h (q c)") for m in range(STACKS)])

            for n_l, l in enumerate(FOLD_ORDER):
                for i, (first, _) in enumerate(W2_PIECES):
                    if l == first:
                        pe.wait_ge(w2_in[i], 16)
                bank = (FOLD_BANK + n_l) % BANKS
                if n_l >= BANKS:
                    pe.wait_ge(fold_used, n_l - BANKS + 1)
                elif bank < FOLD_BANK:
                    pe.wait_ge(w1_used, bank + 1)
                for at, weights in parts_of(l):
                    last = nc.tensor.matmul(tri_ps[:, bank, at:at + weights.shape[1]], w2_sb[:, l, :], weights,
                                            start=True, stop=True)
                last.then_inc(fold_ps, 1)

            pe.wait_ge(dense_in, 16)
            pe.wait_ge(dense_w_in, 16)
            for m in range(TOP1 // P):
                nc.tensor.matmul(tower_ps[m][:, 0:(TILES - 1) * P], wt1d_sb[:, m * P:(m + 1) * P],
                                 dense_sb[:, 0:(TILES - 1) * P], start=True, stop=True).then_inc(dense_ready, 1)

            def transpose_group(bank, t, a, b):
                for l in range(a, b):
                    last = nc.tensor.transpose(bank[0:ROWS[t], (l - a) * H:(l - a + 1) * H],
                                               fold_t[t][:, l - FROM[t], :], ident[:])
                return last

            pe.wait_ge(added, MIDDLE_ADDED)
            pe.wait_ge(zeroed, 1)
            for g, (a, b) in enumerate(EARLY_GROUPS):
                pe.wait_ge(dense_used, g + 1)
                transpose_group(tower_ps[g], HIGH, a, b).then_inc(early_ps, 1)
            pe.wait_ge(dense_used, TOP1 // P)
            pe.wait_ge(early_used, len(EARLY_GROUPS))
            for g, (a, b) in enumerate(LOW_GROUPS):
                if g == 0:
                    pe.wait_ge(added, LOWEST_ADDED)
                if g == LOWEST_GROUPS:
                    pe.wait_ge(added, LOW_ADDED)
                if g >= len(tower_ps):
                    pe.wait_ge(low_used, g - len(tower_ps) + 1)
                transpose_group(tower_ps[g % len(tower_ps)], LOW, a, b).then_inc(low_ps, 1)
            pe.wait_ge(fold_used, FIELDS)

            def make_triples(n, t, runs=range(RUNS)):
                pe.wait_ge(pairs_ready, n * 2 + (t + 1))
                if t == LOW:
                    pe.wait_ge(diag_ready, n + 1)
                    if type(n) is int:
                        pe.wait_ge(diag_shared, 1)
                width = GROUPS * THIRD
                for r in runs:
                    run = t * RUNS + r
                    if not (type(n) is int and run < BANKS):
                        pe.wait_ge(tri_used, n * (2 * RUNS) + (run - BANKS + 1))
                    for q in range(PER_BANK):
                        s = r * PER_BANK + q
                        last = nc.tensor.matmul(
                            tri_ps[0:ROWS[t], run % BANKS, q * width:(q + 1) * width],
                            pairs[:, START[t]:START[t + 1], s],
                            diag[:, s, :, :].rearrange("p g l -> p (g l)"), start=True, stop=True)
                    last.then_inc(tri_ready, 1)

            def make_z(n):
                for t in (LOW, HIGH):
                    pe.wait_ge(tri_used, n * (2 * RUNS) + RUNS * (t + 1))
                    for l in THIRDS[t]:
                        last = nc.tensor.matmul(z_ps[:, 0:P], fold[0:ROWS[t], t, l, :], triples[0:ROWS[t], t, l, :],
                                                start=(t == LOW and l == FROM[t]), stop=(t == HIGH and l == FIELDS - 1))
                        if t == HIGH and l == FIELDS - 1:
                            last.then_inc(z_ready, 1)
                for t in (LOW, HIGH):
                    nc.tensor.matmul(z1_ps, w1p[0:SUMMED[t], t, :], triples[0:SUMMED[t], t, ONE, :],
                                     start=(t == LOW), stop=False)
                pe.wait_ge(stack_made, n + 1)
                for m in range(STACKS):
                    last = nc.tensor.matmul(z1_ps, w1x[:, m, :], stacked[:, m, :],
                                            start=False, stop=(m == STACKS - 1))
                last.then_inc(z_ready, 1)

            def layer1(n):
                shared = type(n) is int
                dense_n = dense_sb[:, (TILES - 1) * P:TILES * P]
                parts = range(3) if shared else (1, 2)
                for part in parts:
                    if part:
                        pe.wait_ge(z_used, n * 2 + part)
                    for m in range(TOP1 // P):
                        cols = slice(m * P, (m + 1) * P)
                        weight, x = [(wt1d_sb[:, cols], dense_n), (wt1_sb[:, 1, cols], z_sb[:, 1, :]),
                                     (wt1_sb[:, 0, cols], z_sb[:, 0, :])][part]
                        bank = h1_dve_ps if shared and m >= TOP1 // P // 2 else h1_ps
                        first = m in ((0, TOP1 // P // 2) if shared else (0,))
                        last = nc.tensor.matmul(bank[:, cols], weight, x, start=(part == parts[0] and first),
                                                stop=(part == 2), skip_group_check=True)
                last.then_inc(h1_ready, 1)

            def layer2(n):
                shared = type(n) is int
                order = [0, 2, 1, 3] if shared else list(range(TOP1 // P))
                if not shared:
                    pe.wait_ge(h1_used, n + 1)
                for c in order:
                    if shared and c < TOP1 // P // 2:
                        pe.wait_ge(h1_used, TILES + c)
                    if shared and c >= TOP1 // P // 2:
                        pe.wait_ge(h1_used_dve, c - TOP1 // P // 2 + 1)
                    for m in range(TOP2 // P):
                        bank = h2_dve_ps if shared and m >= TOP2 // P // 2 else h2_ps
                        last = nc.tensor.matmul(bank[:, m * P:(m + 1) * P], wt2_sb[:, c, m * P:(m + 1) * P],
                                                h1_sb[:, c, :], start=(c == 0 and (m == 0 or shared)),
                                                stop=(c == order[-1]), skip_group_check=True)
                last.then_inc(h2_ready, 1)

            def layer3(n):
                pe.wait_ge(h2_used, n + 1)
                for c in range(TOP2 // P):
                    if type(n) is int and c == TOP2 // P // 2:
                        pe.wait_ge(h2_used_dve, 1)
                    last = nc.tensor.matmul(y_ps[0:1, 0:P], wt3_sb[:, c:c + 1], h2_sb[:, c, :],
                                            start=(c == 0), stop=(c == TOP2 // P - 1))
                last.then_inc(y_ready, 1)

            make_triples(0, LOW)
            make_triples(0, HIGH, range(0, RUNS // 2))

            pe.wait_ge(added, HIGH_ADDED)
            pe.wait_ge(low_used, len(LOW_GROUPS))
            for g, (a, b) in enumerate(HIGH_GROUPS):
                transpose_group(tower_ps[g], HIGH, a, b).then_inc(high_ps, 1)
            make_triples(0, HIGH, range(RUNS // 2, RUNS))
            pe.wait_ge(high_used, len(HIGH_GROUPS))
            pe.wait_ge(vecs_in, 16)
            pe.wait_ge(top_in, 32)

            with pe.Fori(0, TILES - 1) as n:
                make_z(n)
                layer1(n)
                make_triples(n + 1, LOW)
                make_triples(n + 1, HIGH, range(0, RUNS // 2))
                layer2(n)
                make_triples(n + 1, HIGH, range(RUNS // 2, RUNS))
                layer3(n)
            make_z(TILES - 1)
            layer1(TILES - 1)
            layer2(TILES - 1)
            layer3(TILES - 1)

        @block.scalar
        def _(act):
            act.dma_start(dense_sb[:], dense).then_inc(dense_in, 16)
            act.dma_start(wt1d_sb[:], wt1[2 * H:2 * H + DENSE, :]).then_inc(dense_w_in, 16)

            act.wait_ge(vecs_in, 16)
            nc.scalar.copy(w1s[:, W1_AT[HIGH] + N_HIGH:W1_AT[HIGH] + N_HIGH + 1], b1_sb).then_inc(biases_made, 1)
            nc.scalar.mul(b2x[:], b2_sb, float(EMB)).then_inc(biases_made, 1)

            act.wait_ge(w1_ps, 1)
            for t in (LOW, HIGH):
                last = nc.scalar.copy(w1p[0:SUMMED[t], t, :], tri_ps[0:SUMMED[t], W1S_BANK, t * H:(t + 1) * H])
            last.then_inc(w1_used, 1)
            act.wait_ge(w1_ps, 2)
            nc.scalar.copy(w1x[:].rearrange("p m h -> p (m h)"),
                           tri_ps[:, W1Q_BANK, 0:STACKS * H]).then_inc(w1_used, 1)

            for n_l, l in enumerate(FOLD_ORDER):
                bank = tri_ps[:, (FOLD_BANK + n_l) % BANKS, :]
                act.wait_ge(fold_ps, n_l + 1)
                if l >= BASE:
                    nc.scalar.copy(fold_t[LOW][:, l - BASE, 0:SUMMED[LOW]], bank[:, LOW_AT:CROSS_AT])
                    if SPLIT <= l < MID_STOP:
                        nc.scalar.copy(fold_t[LOW][:, l - BASE, SUMMED[LOW]:ROWS[LOW]], bank[:, 0:MIDDLE_ROWS])
                        nc.scalar.copy(middle[:, l - SPLIT, :, :].rearrange("h c j -> h (c j)"),
                                       bank[:, BELOW_AT:BELOW_AT + w1m_row.shape[1]])
                else:
                    nc.scalar.copy(below[:, l, :, :].rearrange("h j i -> h (j i)"),
                                   bank[:, BELOW_AT:BELOW_AT + w1b_row.shape[1]])
                    nc.scalar.copy(fold_t[HIGH][:, l, SUMMED[HIGH]:ROWS[HIGH]], bank[:, LOW_AT:LOW_AT + BASE_ROWS])
                nc.scalar.copy(fold_t[HIGH][:, l, N_HIGH:SUMMED[HIGH]], bank[:, 0:FOLDED_HIGH])
                nc.scalar.copy(cross[:, l, :, :].rearrange("h c i -> h (c i)"),
                               bank[:, CROSS_AT:BELOW_AT]).then_inc(fold_used, 1)
            for m in range(TOP1 // P):
                act.wait_ge(dense_ready, m + 1)
                nc.scalar.activation(dense_h1[:, m, :], tower_ps[m][:, 0:(TILES - 1) * P], ACT.Identity,
                                     bias=bt1_sb[:, m:m + 1]).then_inc(dense_used, 1)

            def copy_triples(n, t, runs=range(RUNS)):
                dst = triples[0:ROWS[t], t, FROM[t]:THIRD, :].rearrange("p l (g s) -> p s g l", g=GROUPS)
                for r in runs:
                    run = t * RUNS + r
                    act.wait_ge(tri_ready, n * (2 * RUNS) + (run + 1))
                    nc.scalar.copy(dst[:, r * PER_BANK:(r + 1) * PER_BANK, :, :],
                                   tri_ps[0:ROWS[t], run % BANKS, 0:PER_BANK * GROUPS * THIRD].rearrange(
                                       "p (s g l) -> p s g l", g=GROUPS, l=THIRD)[:, :, :, FROM[t]:THIRD]).then_inc(tri_used, 1)

            def stack(n):
                act.wait_ge(tri_used, n * (2 * RUNS) + 2 * RUNS)
                for q in range(4):
                    m = len(range(q, N_LOW, 4))
                    last = nc.scalar.copy(stacked[QUAD * q:QUAD * q + N_HIGH, 0:m, :],
                                          triples[0:N_HIGH, HIGH, q:N_LOW:4, :])
                last.then_inc(stack_made, 1)

            def copy_z(n):
                act.wait_ge(z_ready, n * 2 + 1)
                nc.scalar.activation(z_sb[:, 1, :], z_ps[:, 0:P], ACT.Identity,
                                     bias=b2x[:, 0:1]).then_inc(z_used, 1)
                act.wait_ge(z_ready, n * 2 + 2)
                nc.scalar.copy(z_sb[:, 0, :], z1_ps).then_inc(z_used, 1)

            def hidden1(n):
                act.wait_ge(h1_summed, n + 1)
                nc.scalar.activation(h1_sb[:].rearrange("p m r -> p (m r)"), h1_sum[:].rearrange("p m r -> p (m r)"),
                                     ACT.Relu).then_inc(h1_used, 1)

            def hidden1_last():
                act.wait_ge(h1_ready, TILES)
                for m in range(TOP1 // P // 2):
                    nc.scalar.activation(h1_sb[:, m, :], h1_ps[:, m * P:(m + 1) * P], ACT.Relu,
                                         bias=bt1_sb[:, m:m + 1]).then_inc(h1_used, 1)

            def hidden2(n, chunks=range(TOP2 // P)):
                act.wait_ge(h2_ready, n + 1)
                for m in chunks:
                    last = nc.scalar.activation(h2_sb[:, m, :], h2_ps[:, m * P:(m + 1) * P], ACT.Relu,
                                                bias=bt2_sb[:, m:m + 1])
                last.then_inc(h2_used, 1)

            def copy_y(n):
                act.wait_ge(y_ready, n + 1)
                y_n = y_sb[:, n * P:(n + 1) * P] if type(n) is int else y_sb[:, bass.ds(n * P, P)]
                nc.scalar.copy(y_n, y_ps[0:1, 0:P]).then_inc(y_used, 1)

            for g, (a, b) in enumerate(EARLY_GROUPS):
                act.wait_ge(early_ps, g + 1)
                nc.scalar.copy(fold[0:ROWS[HIGH], HIGH, a:b, :].rearrange("p l h -> p (l h)"),
                               tower_ps[g][0:ROWS[HIGH], 0:(b - a) * H]).then_inc(early_used, 1)
            act.wait_ge(cleared, 2)
            act.wait_ge(emb_ready, 1)
            spread_diag(nc.scalar.copy, range(GROUPS), 0, SPLIT)
            for g, (a, b) in enumerate(LOW_GROUPS):
                if g == LOWEST_GROUPS:
                    for part in (1, 2):
                        act.wait_ge(emb_ready, part + 1)
                        last = spread_diag(nc.scalar.copy, range(BY_DVE, GROUPS), *PARTS[part])
                    last.then_inc(diag_shared, 1)
                act.wait_ge(low_ps, g + 1)
                nc.scalar.copy(fold[0:ROWS[LOW], LOW, a:b, :].rearrange("p l h -> p (l h)"),
                               tower_ps[g % len(tower_ps)][0:ROWS[LOW], 0:(b - a) * H]).then_inc(low_used, 1)

            copy_triples(0, LOW)
            copy_triples(0, HIGH, range(0, RUNS // 2))
            copy_triples(0, HIGH, range(RUNS // 2, RUNS))
            act.wait_ge(zeroed, 1)
            stack(0)

            with act.Fori(0, TILES - 1) as n:
                copy_z(n)
                copy_triples(n + 1, LOW)
                hidden1(n)
                copy_triples(n + 1, HIGH, range(0, RUNS // 2))
                hidden2(n)
                copy_triples(n + 1, HIGH, range(RUNS // 2, RUNS))
                stack(n + 1)
                copy_y(n)
            copy_z(TILES - 1)
            hidden1_last()
            hidden2(TILES - 1, range(TOP2 // P // 2))
            copy_y(TILES - 1)


def kernel(**inputs):
    import numpy as np
    import concourse.bacc as bacc
    from concourse.bass_utils import run_bass_kernel_spmd as run

    nc = bacc.Bacc("TRN2", target_bir_lowering=False, num_devices=1)
    arrays = {}

    def arg(name, array=None):
        a = np.ascontiguousarray(inputs[name] if array is None else array)
        arrays["in_" + name] = a
        return nc.dram_tensor("in_" + name, a.shape, mybir.dt.from_np(a.dtype), kind="ExternalInput").ap()

    vecs = [np.asarray(inputs[name]).reshape(-1, P) for name in ("b_top1", "b_top2", "W_top3", "L0_rec_b1", "L0_rec_b2")]
    args = [arg("ids"), [arg(f"tbl_{f}") for f in range(FIELDS)], arg("vectors", np.concatenate(vecs).T)]
    args += [arg("dense_ctx", np.asarray(inputs["dense_ctx"]).T), arg("L0_rec_W1"),
             arg("L0_rec_W2", np.asarray(inputs["L0_rec_W2"]).transpose(1, 2, 0))]
    args += [arg("W_top1"), arg("W_top2")]
    out = nc.dram_tensor("out_y", (BATCH, 1), mybir.dt.float32, kind="ExternalOutput").ap()
    build(nc, *args, out)
    r = run(nc, [arrays], core_ids=[0])
    return r.results[0]["out_y"]
```
